# Optimizing a Trainium2 kernel written in Bass

```python
import numpy as np
import jax
import jax.numpy as jnp

def _softmax(x, axis=-1):
    return jax.nn.softmax(x, axis=axis)
def _gelu(x):
    return jax.nn.gelu(x, approximate=True)
def _silu(x):
    return jax.nn.silu(x)
def _sigmoid(x):
    return jax.nn.sigmoid(x)
def _layernorm(x, axis=-1, eps=1e-5):
    m = jnp.mean(x, axis=axis, keepdims=True)
    v = jnp.var(x, axis=axis, keepdims=True)
    return (x - m) / jnp.sqrt(v + eps)
def _scatter_add(tgt, idx, src, axis=0):
    return tgt.at[idx].add(src)
def _segment_sum(src, seg, n):
    return jax.ops.segment_sum(src, seg, n)

kernel_name = 'mk_conv_preact_d2_conv_nchw32_5519da'

def setup_inputs(seed: int = 0):
    np.random.seed(seed)
    _w = jnp.asarray
    def _rec_inputs():
        import jax
        import jax.numpy as jnp
        _gk = jax.random.key(seed)
        x = -7.109e-05 + 0.9999 * jax.random.normal(jax.random.fold_in(_gk, 1), (8, 32, 512, 512), jnp.float32)
        return x
    x = _rec_inputs()
    def _L0_conv_setup():
        import jax, jax.numpy as jnp
        import numpy as np
        key = jax.random.key(seed)
        k1, k2, k3, k4 = jax.random.split(key, 4)
        B, Cin, Cout, R = (8, 32, 32, 32)
        H, W = (512, 512)
        M1, M2 = (32, 32)
        return {'x': jax.random.normal(k1, (B, Cin, H, W), dtype=jnp.float32), 'coeff_real': jax.random.normal(k2, (R, M1, M2, Cin), dtype=jnp.float32), 'coeff_imag': jax.random.normal(k3, (R, M1, M2, Cin), dtype=jnp.float32), 'proj': jax.random.normal(k4, (Cout, R), dtype=jnp.float32)}
    _L0_conv_all = _L0_conv_setup()
    _L0_conv_in = {k: v for k, v in _L0_conv_all.items() if k in ('coeff_real', 'coeff_imag', 'proj', )}
    del _L0_conv_all

    def _L1_conv_setup():
        import jax, jax.numpy as jnp
        import numpy as np
        B, CIN, COUT, H, W, MODES = (16, 32, 32, 256, 256, 12)
        SCALE = 1.0 / (CIN * COUT)
        key = jax.random.key(seed)
        ks = jax.random.split(key, 5)
        x = jax.random.normal(ks[0], (B, CIN, H, W), dtype=jnp.float32)
        w1_real = SCALE * jax.random.uniform(ks[1], (CIN, COUT, MODES, MODES), dtype=jnp.float32)
        w1_imag = SCALE * jax.random.uniform(ks[2], (CIN, COUT, MODES, MODES), dtype=jnp.float32)
        w2_real = SCALE * jax.random.uniform(ks[3], (CIN, COUT, MODES, MODES), dtype=jnp.float32)
        w2_imag = SCALE * jax.random.uniform(ks[4], (CIN, COUT, MODES, MODES), dtype=jnp.float32)
        return {'x': x, 'w1_real': w1_real, 'w1_imag': w1_imag, 'w2_real': w2_real, 'w2_imag': w2_imag}
    _L1_conv_all = _L1_conv_setup()
    _L1_conv_in = {k: v for k, v in _L1_conv_all.items() if k in ('w1_real', 'w1_imag', 'w2_real', 'w2_imag', )}
    del _L1_conv_all

    return {
        "x": x,
        "L0_conv_coeff_real": _L0_conv_in["coeff_real"],
        "L0_conv_coeff_imag": _L0_conv_in["coeff_imag"],
        "L0_conv_proj": _L0_conv_in["proj"],
        "L1_conv_w1_real": _L1_conv_in["w1_real"],
        "L1_conv_w1_imag": _L1_conv_in["w1_imag"],
        "L1_conv_w2_real": _L1_conv_in["w2_real"],
        "L1_conv_w2_imag": _L1_conv_in["w2_imag"],
    }

def reference(x, L0_conv_coeff_real, L0_conv_coeff_imag, L0_conv_proj, L1_conv_w1_real, L1_conv_w1_imag, L1_conv_w2_real, L1_conv_w2_imag):
    import jax
    import jax.numpy as jnp
    def _L0_conv_ref(x, coeff_real, coeff_imag, proj):
        import jax, jax.numpy as jnp
        import numpy as np
        M1, M2 = (coeff_real.shape[1], coeff_real.shape[2])
        B, Cin, H, W = x.shape
        Cout = proj.shape[0]
        Wc = jnp.einsum('or,rijc->oijc', proj, coeff_real) + 1j * jnp.einsum('or,rijc->oijc', proj, coeff_imag)
        x_ft = jnp.fft.rfftn(x, axes=(-2, -1))
        m1 = min(M1, x_ft.shape[-2])
        m2 = min(M2, x_ft.shape[-1])
        out_modes = jnp.einsum('bcij,oijc->boij', x_ft[:, :, :m1, :m2], Wc[:, :m1, :m2, :])
        out_ft = jnp.zeros((B, Cout, H, x_ft.shape[-1]), dtype=x_ft.dtype)
        out_ft = out_ft.at[:, :, :m1, :m2].set(out_modes)
        return jnp.fft.irfftn(out_ft, s=(H, W), axes=(-2, -1))

    def _L1_conv_ref(x, w1_real, w1_imag, w2_real, w2_imag):
        import jax, jax.numpy as jnp
        import numpy as np
        B, CIN, COUT, H, W, MODES = (16, 32, 32, 256, 256, 12)
        SCALE = 1.0 / (CIN * COUT)
        m = MODES
        w1 = w1_real + 1j * w1_imag
        w2 = w2_real + 1j * w2_imag
        x_ft = jnp.fft.rfft2(x)
        lo = jnp.einsum('bixy,ioxy->boxy', x_ft[:, :, :m, :m], w1)
        hi = jnp.einsum('bixy,ioxy->boxy', x_ft[:, :, -m:, :m], w2)
        out_ft = jnp.zeros((x.shape[0], COUT, x.shape[-2], x.shape[-1] // 2 + 1), dtype=jnp.complex64)
        out_ft = out_ft.at[:, :, :m, :m].set(lo)
        out_ft = out_ft.at[:, :, -m:, :m].set(hi)
        return jnp.fft.irfft2(out_ft, s=(x.shape[-2], x.shape[-1]))

    def _gn(v, G=16, eps=1e-5):
        B_, C_, H_, W_ = v.shape
        g = v.reshape(B_, G, C_ // G, H_, W_)
        m = jnp.mean(g, axis=(2, 3, 4), keepdims=True)
        s = jnp.var(g, axis=(2, 3, 4), keepdims=True)
        return ((g - m) / jnp.sqrt(s + eps)).reshape(v.shape)

    def _ln_c(v, eps=1e-6):
        m = jnp.mean(v, axis=1, keepdims=True)
        s = jnp.var(v, axis=1, keepdims=True)
        return (v - m) / jnp.sqrt(s + eps)

    def _ln_t(v, eps=1e-5):
        m = jnp.mean(v, axis=-1, keepdims=True)
        s = jnp.var(v, axis=-1, keepdims=True)
        return (v - m) / jnp.sqrt(s + eps)

    def _to_tokens(v):
        B_, C_, H_, W_ = v.shape
        return v.reshape(B_, C_, H_ * W_).transpose(0, 2, 1)
    def _from_tokens(t, like):
        B_, C_, H_, W_ = like.shape
        return t.transpose(0, 2, 1).reshape(B_, C_, H_, W_)

    x = x + _L0_conv_ref(_gn(x), L0_conv_coeff_real, L0_conv_coeff_imag, L0_conv_proj)
    x = x + _L1_conv_ref(_gn(x), L1_conv_w1_real, L1_conv_w1_imag, L1_conv_w2_real, L1_conv_w2_imag)
    return x


_drawn_inputs = setup_inputs


def setup_inputs(seed=0):
    import zlib

    import numpy as np

    out = dict(_drawn_inputs(seed))
    spreads = {}
    factors = {'L1_conv_w1_real': 200.0,
     'L1_conv_w1_imag': 200.0,
     'L1_conv_w2_real': 200.0,
     'L1_conv_w2_imag': 200.0}
    for name, (base, spread) in spreads.items():
        noise = np.random.default_rng([zlib.crc32(name.encode()), seed]).standard_normal(out[name].shape)
        drawn = base * np.exp(spread * noise) if base else spread * noise
        out[name] = jnp.asarray(drawn.astype(out[name].dtype))
    for name, factor in factors.items():
        out[name] = (out[name] * factor).astype(out[name].dtype)
    return out
```

```python
import math

import numpy as np

import concourse.bass as bass
from concourse import mybir
from contextlib import ExitStack

FP32 = mybir.dt.float32
BF16 = mybir.dt.bfloat16
ALU = mybir.AluOpType
ACT = mybir.ActivationFunctionType
AX = mybir.AxisListType

B, C, H, W = 8, 32, 512, 512
K0 = 32
K1 = 12
M1 = 2 * K1
P = 128
NJ = H // P
NW = W // P
NP = C // 2
NQ = 4
PQ = NP // NQ
HO = C // 2
GROUP = 2 * H * W
EPS = 1e-5

MATS = ["rc", "rs", "rcn", "dc", "ah", "ahr0", "ahi0", "rc1", "rs1", "rcn1", "s1", "s1r0", "s1i0",
        "qc", "qs", "qsn", "pc", "ps", "psn", "ident"]
MAT_AT = {name: n * P for n, name in enumerate(MATS)}
SUMS = ["ones", "sums", "w8", "w4", "ysum"]
SUM_AT = {name: len(MATS) * P + n for n, name in enumerate(SUMS)}
ROW_DFT = len(MATS) * P + 8
COL_DFT = ROW_DFT + NJ * 2 * K0
ROW_INV = COL_DFT + NW * 2 * K0
COL_INV = ROW_INV + H
NCONST = COL_INV + W


def constants():
    t = np.zeros((P, NCONST), np.float64)

    def z(i, cs, k):
        return 64 * i + 32 * cs + k

    def g(o, i, k):
        return 64 * o + 32 * i + k

    def put(name, row, col, v):
        t[row, MAT_AT[name] + col] += v

    for i in range(2):
        for o in range(2):
            for k in range(K0):
                put("rc", z(i, 0, k), g(o, i, k), 1)
                put("rcn", z(i, 0, k), g(o, i, k), -1)
                put("rs", z(i, 1, k), g(o, i, k), -1)
            for i2 in range(2):
                put("dc", z(i2, 0, 0), g(o, i, 0), -0.5)
            for m in range(M1):
                j, sign = (m, -1) if m < K1 else (M1 - m, 1)
                put("rc1", z(i, 0, j), g(o, i, m), 1)
                put("rcn1", z(i, 0, j), g(o, i, m), -1)
                put("rs1", z(i, 1, j), g(o, i, m), sign)
    for o in range(2):
        for i in range(2):
            for rep in range(2):
                for k in range(K0):
                    put("ah", g(o, i, k), g(rep, o, k), 0.5)
                    put("ahr0", g(o, i, k), g(rep, o, k), 0.25 if k else 0.5)
                    put("ahi0", g(o, i, k), g(rep, o, k), 0.25 if k else 0)
                for m in range(K1):
                    put("s1", g(o, i, m), g(rep, o, m), 1)
                for m in range(1, K1):
                    put("s1r0", g(o, i, m), g(rep, o, m), 0.5)
                    put("s1i0", g(o, i, m), g(rep, o, m), 0.5)
                for m in range(K1, M1):
                    put("s1r0", g(o, i, M1 - m), g(rep, o, m), 0.5)
                    put("s1i0", g(o, i, M1 - m), g(rep, o, m), -0.5)
                for i2 in range(2):
                    put("s1r0", g(o, i, 0), g(rep, i2, 0), 0.5 if i2 == o else -0.5)
            for k in range(K0):
                put("qc", g(o, i, k), k, 1)
                put("qs", g(o, i, k), 64 + k, 1)
                put("qsn", g(o, i, k), 64 + k, -1)
            for m in range(M1):
                r = m if m < K1 else K0 + m - K1
                put("pc", g(o, i, m), r, 1)
                put("ps", g(o, i, m), 64 + r, 1)
                put("psn", g(o, i, m), 64 + r, -1)
    t[:, SUM_AT["ones"]] = 1
    t[:, MAT_AT["ident"]:MAT_AT["ident"] + P] = np.eye(P)
    for i in range(2):
        t[z(i, 0, 0), SUM_AT["sums"]] = 1
        t[g(0, i, 0), SUM_AT["w4"]] = -4
        t[g(0, i, 0), SUM_AT["ysum"]] = 2
    t[0:64, SUM_AT["w8"]] = 8

    def angle(a, b, n):
        return 2 * np.pi * np.mod(np.multiply.outer(a, b), n) / n

    part, kx = np.arange(P), np.arange(K0)
    for j in range(NJ):
        a = angle(NJ * part + j, kx, H)
        t[:, ROW_DFT + 64 * j:ROW_DFT + 64 * j + 64] = np.concatenate([np.cos(a), np.sin(a)], 1)
        a = angle(P * j + part, kx, W)
        t[:, COL_DFT + 64 * j:COL_DFT + 64 * j + 64] = np.concatenate([np.cos(a), np.sin(a)], 1)
        rows = np.concatenate([kx, np.arange(H - K1, H)])
        a = angle(rows, NJ * part + j, H)
        t[0:K0 + K1, ROW_INV + P * j:ROW_INV + P * j + P] = np.cos(a)
        t[64:64 + K0 + K1, ROW_INV + P * j:ROW_INV + P * j + P] = np.sin(a)
    gain = np.where(kx == 0, 1.0, 2.0)[:, None] / (H * W)
    a = angle(kx, np.arange(W), W)
    for i in range(2):
        t[64 * i:64 * i + 32, COL_INV:COL_INV + W] = gain * np.cos(a)
        t[64 * i + 32:64 * i + 64, COL_INV:COL_INV + W] = -gain * np.sin(a)
    return t.astype(np.float32)


STEPS = NP
QUAD_STEP = [7, 10, 13]
QUAD_CHUNKS = [[2, 1, 1], [2, 1, 1], [2, 1, 1]]
LAST_QUAD_STEP, CROSS_STEP, CC_STEP, L1_STEP, PV_STEP = 1, 3, 4, 5, 9
PASS2 = {10: 3, 11: 3, 12: 3, 13: 3, 14: 2, 15: 2}
assert sum(PASS2.values()) == NP
NO4 = 4
NO2 = 2
NY = 4
U1 = HO // NO2


def conv_preact_two_layers(nc, x, coeff_re, coeff_im, proj, w1_re, w1_im, w2_re, w2_im, table, out):
    xv = x.rearrange("b c (p j) w -> b c p (j w)", j=NJ)
    ov = out.rearrange("b c (p j) w -> b c p (j w)", j=NJ)

    ctx = ExitStack()
    with ctx:
        def sb(name, shape, dt=FP32):
            return ctx.enter_context(nc.sbuf_tensor(name, shape, dt))

        def sem(name):
            return ctx.enter_context(nc.semaphore(name))

        def view(t, offset, dims, parts=P, part0=0):
            row = t[:].ap[0][0]
            return bass.AP(tensor=t[:].tensor, offset=part0 * row + offset, ap=[[row, parts], *dims])

        const = sb("const", [P, NCONST])
        w0 = sb("w0", [P, HO, NQ, K0, 2, PQ])
        w1 = sb("w1", [P, HO, 2, NP, K1])
        x1 = sb("x1", [P, 4, NJ * W])
        x2 = sb("x2", [P, 4, NJ * W])
        rows = sb("rows", [P, W])
        cols = sb("cols", [P, NW, P])
        zq = sb("zq", [P, 2 * PQ, 2, K0])
        xt = sb("xt", [P, 2, NP, K0])
        xb = sb("xb", [P, 2, NP, K1])
        junk = sb("junk", [P, 2, 1024], BF16)
        sq = sb("sq", [P, NP, 4])
        prod_v = sb("prod_v", [P, 1024])
        prod_g = sb("prod_g", [P, 2, 1024])
        tacc = sb("tacc", [P, 2, HO, K0])
        tq = sb("tq", [P, 2, 2, NO4, K0])
        xab = sb("xab", [P, 2, K0, 2, PQ])
        xab1 = sb("xab1", [P, 2, 2, NP, K1])
        vacc = sb("vacc", [P, 2, HO, K1])
        csb = sb("csb", [P, NP, 2, 2, K0])
        gsb = sb("gsb", [P, 2, H])
        st = sb("st", [P, 5, PQ])
        var0 = sb("var0", [P, NP])
        rr0 = sb("rr0", [P, 2, PQ])
        st1 = sb("st1", [P, 4, NP])
        rr1 = sb("rr1", [P, 2, NP])
        dq = sb("dq", [P, 2, NP])
        expo = sb("expo", [P, NP])
        ah = csb[:, 0:8, :, :, :].rearrange("p a i r k -> p (a i r k)").rearrange("p (r n) -> p r n", r=2)

        def bank(name):
            return ctx.enter_context(nc.psum_tensor(name, [P, 512], FP32))

        fa = bank("fa")
        ft = bank("ft")
        zb = bank("zb")
        mid = bank("mid")
        yb = [bank(f"y{n}") for n in range(NY)]

        def mat(name):
            return const[:, MAT_AT[name]:MAT_AT[name] + P]

        def total(name):
            return const[:, SUM_AT[name]:SUM_AT[name] + 1].broadcast_to([P, P])

        def half(name, o):
            return const[64 * o:64 * o + 64, MAT_AT[name]:MAT_AT[name] + P]

        row_dft = const[:, ROW_DFT:COL_DFT].rearrange("p (j n) -> p j n", j=NJ)
        col_dft = const[:, COL_DFT:ROW_INV].rearrange("p (j n) -> p j n", j=NW)
        row_inv = const[:, ROW_INV:COL_INV]
        col_inv = const[:, COL_INV:NCONST]

        coef = [x2[:, n, :].rearrange("p (r n) -> p r n", r=2) for n in (0, 1)]
        wst = [x2[:, n, :].rearrange("p (i q k s c) -> p i q k s c", i=2, q=NQ, k=K0, s=2) for n in (2, 3)]
        projb = prod_g[:, 0, 0:P]

        s_const = sem("s_const")
        s_zero = sem("s_zero")
        s_proj = sem("s_proj")
        s_w1 = sem("s_w1")
        s_coef = [sem("s_coef0"), sem("s_coef1")]
        s_wc = sem("s_wc")
        s_wst = sem("s_wst")
        s_w0 = [sem("s_w0a"), sem("s_w0b")]
        s_x1 = [sem(f"s_x1_{n}") for n in range(4)]
        s_x2 = [sem(f"s_x2_{n}") for n in range(4)]
        s_out = [sem(f"s_out_{n}") for n in range(4)]
        s_fa = sem("s_fa")
        s_sq = sem("s_sq")
        s_junk = sem("s_junk")
        s_rows = sem("s_rows")
        s_ft = sem("s_ft")
        s_cols = sem("s_cols")
        s_zb = sem("s_zb")
        s_zq = sem("s_zq")
        s_quad = sem("s_quad")
        s_keep = sem("s_keep")
        s_st = sem("s_st")
        s_rs = sem("s_rs")
        s_rr = sem("s_rr")
        s_xab = sem("s_xab")
        s_pv0 = sem("s_pv0")
        s_pg0 = sem("s_pg0")
        s_red = sem("s_red")
        s_tacc = sem("s_tacc")
        s_cross = sem("s_cross")
        s_ah = sem("s_ah")
        s_cadd = sem("s_cadd")
        s_cmul = sem("s_cmul")
        s_cred = sem("s_cred")
        s_tot = sem("s_tot")
        s_st1 = sem("s_st1")
        s_rs1 = sem("s_rs1")
        s_rr1 = sem("s_rr1")
        s_cc = sem("s_cc")
        s_ccc = sem("s_ccc")
        s_l1 = sem("s_l1")
        s_x1s = sem("s_x1s")
        s_xab1 = sem("s_xab1")
        s_pv1 = sem("s_pv1")
        s_pg1 = sem("s_pg1")
        s_red1 = sem("s_red1")
        s_pv = sem("s_pv")
        s_cs = sem("s_cs")
        s_gp = sem("s_gp")
        s_gs = sem("s_gs")
        s_y = sem("s_y")
        s_add = sem("s_add")

        block = ctx.enter_context(nc.Block())

        def is_zero(b):
            return isinstance(b, int) and b == 0

        def pass2_pairs(s):
            first = sum(n for step, n in PASS2.items() if step < s)
            return range(first, first + PASS2.get(s, 0))

        def quad_chunks(s):
            for q, start in enumerate(QUAD_STEP):
                done = 0
                for n, count in enumerate(QUAD_CHUNKS[q]):
                    for t in range(done, done + count):
                        if s == start + n:
                            yield q, t
                    done += count

        @block.sync
        def _(sp):
            def load_pass1(b, s):
                if s >= 2 or not is_zero(b):
                    sp.wait_ge(s_fa, b * NP + s - 1)
                    sp.wait_ge(s_sq, b * NP + s - 1)
                for m in (2 * s, 2 * s + 1):
                    sp.dma_start(x1[:, m % 4, :], xv[b, m]).then_inc(s_x1[m % 4], 16)

            def load_pass2(a, k):
                for m in (2 * k, 2 * k + 1):
                    n = m % 4
                    if m >= 4 or not is_zero(a):
                        sp.wait_ge(s_out[n], a * 128 + 16 * (m // 4))
                    sp.dma_start(x2[:, n, :], xv[a, m]).then_inc(s_x2[n], 16)

            sp.dma_start(const[:, :], table).then_inc(s_const, 16)

            def load_coef(k):
                n = k % 2
                if k >= 2:
                    sp.wait_ge(s_wc, 4 * (k - 1))
                for r, src in enumerate((coeff_re, coeff_im)):
                    for kg in range(4):
                        sp.dma_start(coef[n][32 * kg:32 * kg + 32, r, :],
                                     src[:, 8 * kg + k].rearrange("r j c -> r (j c)")).then_inc(s_coef[n], 16)

            def scatter_w0(k):
                sp.wait_ge(s_wst, 8 * (k + 1))
                for kg in range(4):
                    for o in range(2):
                        for i in range(2):
                            part = 64 * o + 32 * i + 8 * kg + k
                            src = wst[k % 2][32 * kg + o:32 * kg + 32:2, i].rearrange("p q k s c -> p (q k s c)")
                            dst = w0[part:part + 1].rearrange("p o q k s c -> p o (q k s c)")
                            sp.dma_start(dst, src).then_inc(s_w0[k % 2], 16)

            def body(b):
                for s in range(STEPS):
                    load_pass1(b, s)
                    for k in pass2_pairs(s):
                        load_pass2(b - 1, k)

            load_pass1(0, 0)
            load_coef(0)
            load_coef(1)
            for s in range(STEPS):
                if s + 1 < STEPS:
                    load_pass1(0, s + 1)
                if s < 8:
                    scatter_w0(s)
                    if s + 2 < 8:
                        load_coef(s + 2)
            sp.wait_ge(s_w0[0], 64 * 16)
            sp.wait_ge(s_w0[1], 64 * 16)
            body(1)
            with sp.Fori(2, B) as b:
                body(b)
            for k in range(NP):
                load_pass2(B - 1, k)

        @block.tensor
        def _(pe):
            def wc_products(k):
                pe.wait_ge(s_coef[k % 2], 8 * 16 * (k // 2 + 1))
                for r in range(2):
                    for hh in range(2):
                        u = 4 * k + 2 * r + hh
                        if u >= NY:
                            pe.wait_ge(s_wst, 2 * (u - NY + 1))
                        nc.tensor.matmul(yb[u % NY][:, :], projb, coef[k % 2][:, r, 512 * hh:512 * hh + 512],
                                         start=True, stop=True).then_inc(s_wc, 1)

            def transposes(b, s):
                pe.wait_ge(s_rows, b * NP + s + 1)
                if s or not is_zero(b):
                    pe.wait_ge(s_cols, b * NP + s)
                for w in range(NW):
                    last = nc.tensor.transpose(ft[:, P * w:P * w + P], rows[:, P * w:P * w + P], mat("ident"))
                last.then_inc(s_ft, 1)

            def row_transform(b, s):
                if s or not is_zero(b):
                    pe.wait_ge(s_rows, b * NP + s)
                for i in range(2):
                    m = 2 * s + i
                    pe.wait_ge(s_x1[m % 4], b * 128 + 16 * (m // 4 + 1))
                for j in range(NJ):
                    for i in range(2):
                        slot = (2 * s + i) % 4
                        last = nc.tensor.matmul(fa[64 * i:64 * i + 64, :], row_dft[:, j, :],
                                                x1[:, slot, W * j:W * j + W],
                                                start=(j == 0), stop=(j == NJ - 1))
                last.then_inc(s_fa, 1)

            def col_transform(b, s):
                pe.wait_ge(s_cols, b * NP + s + 1)
                if s or not is_zero(b):
                    pe.wait_ge(s_zq, b * NP + s)
                for w in range(NW):
                    last = nc.tensor.matmul(zb[:, 0:2 * K0], cols[:, w, :], col_dft[:, w, :],
                                            start=(w == 0), stop=(w == NW - 1))
                last.then_inc(s_zb, 1)

            def quad_spectra(b, q):
                pe.wait_ge(s_zq, b * NP + PQ * (q + 1))
                pe.wait_ge(s_sq, b * NP + PQ * (q + 1))
                if q:
                    pe.wait_ge(s_keep, 2 * (NQ * b + q))
                    pe.wait_ge(s_xab, 2 * (NQ * b + q))
                z = zq[:, PQ * (q % 2):PQ * (q % 2) + PQ]
                nc.tensor.matmul(mid[:, 0:16], total("ones"), sq[:, PQ * q:PQ * q + PQ, :], start=True, stop=True)
                nc.tensor.matmul(mid[:, 16:20], total("sums"), z[:, :, 0, 0], start=True, stop=True)
                for at, n, c, sn, cn in ((128, K0, "rc", "rs", "rcn"), (384, K1, "rc1", "rs1", "rcn1")):
                    re = mid[:, at:at + PQ * n]
                    im = mid[:, at + PQ * n:at + 2 * PQ * n]
                    nc.tensor.matmul(re, mat(c), z[:, :, 0, 0:n], start=True, stop=False)
                    nc.tensor.matmul(re, mat(sn), z[:, :, 1, 0:n], start=False, stop=False)
                    nc.tensor.matmul(re.rearrange("p (a k) -> p a k", k=n)[:, :, 0], mat("dc"), z[:, :, 0, 0],
                                     start=False, stop=True)
                    nc.tensor.matmul(im, mat(sn), z[:, :, 0, 0:n], start=True, stop=False)
                    last = nc.tensor.matmul(im, mat(cn), z[:, :, 1, 0:n], start=False, stop=True)
                last.then_inc(s_quad, 1)

            def cross_spectra(a):
                pe.wait_ge(s_keep, 2 * NQ * (a + 1))
                pe.wait_ge(s_xab, 2 * NQ * (a + 1))
                pe.wait_ge(s_red, 32 * (a + 1))
                pe.wait_ge(s_tacc, 12 * (a + 1))
                for r, col0 in enumerate(("ahr0", "ahi0")):
                    if r:
                        pe.wait_ge(s_ah, 2 * a + 1)
                        pe.wait_ge(s_cadd, 2 * a + 1)
                    m3 = mid[:, :].rearrange("p (a k) -> p a k", k=K0)
                    nc.tensor.matmul(m3[:, :, 1:K0], mat("ah"), tacc[:, r, :, 1:K0], start=True, stop=True)
                    nc.tensor.matmul(m3[:, :, 0], mat(col0), tacc[:, r, :, 0], start=True, stop=True)\
                        .then_inc(s_cross, 1)

            def cross_totals(a):
                pe.wait_ge(s_cred, 2 * (a + 1))
                pe.wait_ge(s_ah, 2 * (a + 1))
                nc.tensor.matmul(mid[:, 0:NP], total("w8"), dq[:, 0, :], start=True, stop=False)
                nc.tensor.matmul(mid[:, 0:NP], total("w8"), dq[:, 1, :], start=False, stop=False)
                p0 = prod_v[:, 0:512].rearrange("p (a k) -> p a k", k=K0)
                nc.tensor.matmul(mid[:, 0:NP], total("w4"), p0[:, :, 0], start=False, stop=True)
                a0 = ah[:, 0, :].rearrange("p (a k) -> p a k", k=K0)
                nc.tensor.matmul(mid[:, NP:2 * NP], total("ysum"), a0[:, :, 0], start=True, stop=True)\
                    .then_inc(s_tot, 1)

            def inverse_input_l0(a):
                for u in range(4):
                    o, r = u // 2, u % 2
                    if u == 0:
                        pe.wait_ge(s_st1, 5 * a + 2)
                    else:
                        pe.wait_ge(s_ccc, 4 * a + u)
                    k = slice(64 * o, 64 * o + 64)
                    nc.tensor.matmul(mid[:, :], half("qc", o), tacc[k, r], start=True, stop=False)
                    nc.tensor.matmul(mid[:, :], half("qs" if r else "qsn", o), tacc[k, 1 - r],
                                     start=False, stop=True).then_inc(s_cc, 1)

            def layer1_input(a):
                pe.wait_ge(s_ccc, 4 * (a + 1))
                for r, col0 in enumerate(("s1r0", "s1i0")):
                    m3 = mid[:, 192 * r:192 * r + 192].rearrange("p (a k) -> p a k", k=K1)
                    nc.tensor.matmul(m3[:, :, 1:K1], mat("s1"), tacc[:, r, :, 1:K1], start=True, stop=True)
                    last = nc.tensor.matmul(m3[:, :, 0], mat(col0), tacc[:, r, :, 0], start=True, stop=True)
                last.then_inc(s_l1, 1)

            def inverse_input_l1(a, after):
                pe.wait_ge(s_red1, 2 * U1 * (a + 1))
                for sem_, count in after:
                    pe.wait_ge(sem_, count)
                for u in range(4):
                    o, r = u // 2, u % 2
                    if u:
                        pe.wait_ge(s_cs, 4 * a + u)
                    k = slice(64 * o, 64 * o + 64)
                    nc.tensor.matmul(mid[:, 0:192], half("pc", o), vacc[k, r], start=True, stop=False)
                    nc.tensor.matmul(mid[:, 0:192], half("ps" if r else "psn", o), vacc[k, 1 - r],
                                     start=False, stop=True).then_inc(s_pv, 1)

            def inverse_rows(a, k, ft_uses):
                if k == 0:
                    pe.wait_ge(s_cs, 4 * (a + 1))
                if k or not is_zero(a):
                    pe.wait_ge(s_gs, a * NP + k)
                pe.wait_ge(s_cols, ft_uses)
                nc.tensor.matmul(ft[:, :], csb[:, k].rearrange("p i r k -> p (i r k)"), row_inv,
                                 start=True, stop=True).then_inc(s_gp, 1)

            def inverse_cols(a, k):
                pe.wait_ge(s_gs, a * NP + k + 1)
                for j in range(NJ):
                    for i in range(2):
                        u = 8 * k + 2 * j + i
                        pe.wait_ge(s_add, a * 128 + max(u - NY + 1, 0))
                        nc.tensor.matmul(yb[u % NY][:, :], gsb[64 * i:64 * i + 64, k % 2, P * j:P * j + P],
                                         col_inv[64 * i:64 * i + 64, :], start=True, stop=True).then_inc(s_y, 1)

            def gp_uses(a, pairs_done):
                if pairs_done or not is_zero(a):
                    pe.wait_ge(s_gs, a * NP + pairs_done)

            def body(b, first, last):
                a = b - 1
                done = 0
                for s in range(STEPS):
                    if s or not first:
                        if not (last and s):
                            if not first:
                                gp_uses(a, done)
                            transposes(b, s - 1)
                    if not last:
                        row_transform(b, s)
                    if s or not first:
                        if not (last and s):
                            col_transform(b, s - 1)
                    if first and s < 8:
                        if s == 0:
                            pe.wait_ge(s_proj, 4 * 16)
                        wc_products(s)
                    if not first:
                        if s == LAST_QUAD_STEP:
                            quad_spectra(a, NQ - 1)
                        if s == CROSS_STEP:
                            cross_spectra(a)
                        if s == CC_STEP:
                            cross_totals(a)
                            inverse_input_l0(a)
                        if s == L1_STEP:
                            layer1_input(a)
                        if s == PV_STEP:
                            nq = NQ * b + 1 if not last else NQ * b
                            inverse_input_l1(a, [(s_keep, 2 * nq), (s_xab, 2 * nq)])
                    if not last and s in QUAD_STEP:
                        q = QUAD_STEP.index(s)
                        if q == 0 and not first:
                            pe.wait_ge(s_x1s, a + 1)
                        if q == 1 and not first:
                            pe.wait_ge(s_cs, 4 * (a + 1))
                        quad_spectra(b, q)
                    if not first:
                        for k in pass2_pairs(s):
                            uses = b * NP + s if not last else b * NP
                            inverse_rows(a, k, uses)
                            inverse_cols(a, k)
                            done = k + 1
            pe.wait_ge(s_const, 16)
            body(0, True, False)
            body(1, False, False)
            with pe.Fori(2, B) as b:
                body(b, False, False)
            body(B, False, True)

        @block.scalar
        def _(act):
            def copy(dst, src):
                return nc.scalar.activation(dst, src, ACT.Copy)

            def squares(b, s):
                for i in range(2):
                    m = 2 * s + i
                    act.wait_ge(s_x1[m % 4], b * 128 + 16 * (m // 4 + 1))
                    if i == 0 and not is_zero(b):
                        act.wait_ge(s_quad, NQ * (b - 1) + s // PQ + 1)
                    for hh in range(2):
                        if i or hh == 0:
                            act.wait_ge(s_junk, 3 * NP * b + 3 * s + 2 * i + hh - (1 if i else 0))
                        else:
                            act.wait_ge(s_sq, NP * b + s)
                        last = nc.scalar.activation(junk[:, hh, :], x1[:, m % 4, 1024 * hh:1024 * hh + 1024], ACT.Square,
                                                    accum_out=sq[:, s, 2 * i + hh:2 * i + hh + 1])
                        if i == 0 or hh == 0:
                            last.then_inc(s_junk, 1)
                last.then_inc(s_sq, 1)

            def copy_rows(b, s):
                act.wait_ge(s_fa, b * NP + s + 1)
                if s or not is_zero(b):
                    act.wait_ge(s_ft, b * NP + s)
                copy(rows[:, :], fa[:, :]).then_inc(s_rows, 1)

            def copy_cols(b, s):
                act.wait_ge(s_ft, b * NP + s + 1)
                if s or not is_zero(b):
                    act.wait_ge(s_zb, b * NP + s)
                copy(cols[:, :, :].rearrange("p a b -> p (a b)"), ft[:, :]).then_inc(s_cols, 1)

            def copy_spectrum(b, s):
                act.wait_ge(s_zb, b * NP + s + 1)
                if s >= 8 or not is_zero(b):
                    act.wait_ge(s_quad, NQ * b + (s - 8) // PQ + 1)
                copy(zq[:, s % (2 * PQ)].rearrange("p t k -> p (t k)"), zb[:, 0:2 * K0]).then_inc(s_zq, 1)

            def keep_quad(b, q):
                act.wait_ge(s_quad, NQ * b + q + 1)
                if q == 0 and not is_zero(b):
                    act.wait_ge(s_xab1, 2 * b)
                for dst, at, n in ((xt, 128, K0), (xb, 384, K1)):
                    copy(dst[:, :, PQ * q:PQ * q + PQ, :],
                         mid[:, at:at + 2 * PQ * n].rearrange("p (r a k) -> p r a k", r=2, k=n)).then_inc(s_keep, 1)

            def copy_cross(a):
                act.wait_ge(s_gp, NP * a)
                for r in range(2):
                    act.wait_ge(s_cross, 2 * a + r + 1)
                    copy(ah[:, r, :], mid[:, :]).then_inc(s_ah, 1)

            def copy_inverse_input(a):
                for u in range(4):
                    o, r = u // 2, u % 2
                    act.wait_ge(s_cc, 4 * a + u + 1)
                    copy(csb[:, :, o, r, :], mid[:, :].rearrange("p (a k) -> p a k", k=K0)).then_inc(s_ccc, 1)

            def copy_inverse_rows(a, k):
                act.wait_ge(s_gp, a * NP + k + 1)
                act.wait_ge(s_y, a * 128 + 8 * max(k - 1, 0))
                copy(gsb[:, k % 2, :], ft[:, :]).then_inc(s_gs, 1)

            def store(a, k):
                for i in range(2):
                    m = 2 * k + i
                    act.wait_ge(s_add, a * 128 + 8 * (k + 1) - 1 + i)
                    act.dma_start(ov[a, m], x2[:, m % 4, :]).then_inc(s_out[m % 4], 16)

            def body(b, first, last):
                a = b - 1
                for s in range(STEPS):
                    if (s or not first) and not (last and s):
                        copy_cols(b, s - 1)
                    if not last:
                        squares(b, s)
                        copy_rows(b, s)
                    if (s or not first) and not (last and s):
                        copy_spectrum(b, s - 1)
                    if not first:
                        if s == LAST_QUAD_STEP:
                            keep_quad(a, NQ - 1)
                        if s == CROSS_STEP:
                            copy_cross(a)
                        if s == CC_STEP:
                            copy_inverse_input(a)
                    if not last and s in QUAD_STEP:
                        keep_quad(b, QUAD_STEP.index(s))
                    if not first:
                        for k in pass2_pairs(s):
                            copy_inverse_rows(a, k)
                            if k:
                                store(a, k - 1)
                if not first:
                    store(a, NP - 1)

            act.wait_ge(s_zero, 2)
            for kg in range(4):
                act.dma_start(prod_g[32 * kg:32 * kg + 32, 0, 32 * kg:32 * kg + 32],
                              proj.rearrange("o r -> r o"), allow_slow_non_contiguous=True).then_inc(s_proj, 16)
            for n, (src, slot) in enumerate(((w1_re, 0), (w1_im, 1), (w2_re, 0), (w2_im, 1))):
                for o in range(2):
                    for i in range(2):
                        part = 64 * o + 32 * i + K1 * (n // 2)
                        for ho in range(HO):
                            act.dma_start(w1[part:part + K1, ho, slot], src[i::2, 2 * ho + o].rearrange("c x y -> x c y"),
                                          allow_slow_non_contiguous=True).then_inc(s_w1, 16)

            body(0, True, False)
            body(1, False, False)
            with act.Fori(2, B) as b:
                body(b, False, False)
            body(B, False, True)
            for n in range(4):
                act.wait_ge(s_out[n], 16 * B * C // 4)

        @block.vector
        def _(dve):
            def to_staging(k):
                if k >= 2:
                    dve.wait_ge(s_w0[k % 2], 16 * 16 * (k // 2))
                for r in range(2):
                    for hh in range(2):
                        u = 4 * k + 2 * r + hh
                        dve.wait_ge(s_wc, u + 1)
                        for i in range(2):
                            src = yb[u % NY][:, :].rearrange("p (k q c i) -> p i q k c", q=NQ, c=PQ, i=2)[:, i]
                            dst = wst[k % 2][:, i, :, 16 * hh:16 * hh + 16, r, :]
                            nc.vector.tensor_copy(dst, src).then_inc(s_wst, 1)

            def quad_statistics(b, q):
                n = NQ * b + q
                dve.wait_ge(s_keep, 2 * (n + 1))
                nc.vector.tensor_reduce(st[:, 0, :], mid[:, 0:16].rearrange("p (a n) -> p a n", n=4), AX.X, ALU.add)\
                    .then_inc(s_st, 1)
                nc.vector.tensor_scalar(st[:, 1, :], mid[:, 16:20], 1.0 / GROUP, None, ALU.mult).then_inc(s_st, 1)
                dve.wait_ge(s_st, 5 * n + 2)
                nc.vector.tensor_tensor(st[:, 2, :], st[:, 1, :], st[:, 1, :], ALU.mult).then_inc(s_st, 1)
                dve.wait_ge(s_st, 5 * n + 3)
                v = var0[:, PQ * q:PQ * q + PQ]
                nc.vector.scalar_tensor_tensor(v, st[:, 0, :], 1.0 / GROUP, st[:, 2, :], ALU.mult, ALU.subtract)\
                    .then_inc(s_st, 1)
                dve.wait_ge(s_st, 5 * n + 4)
                nc.vector.tensor_scalar(st[:, 3, :], v, 0.0, EPS, ALU.max, ALU.add).then_inc(s_st, 1)
                dve.wait_ge(s_rs, n + 1)
                nc.vector.tensor_scalar(rr0[:, 0, :], rr0[:, 1, :], -1.0, None, ALU.mult).then_inc(s_rr, 1)
                if q or not is_zero(b):
                    dve.wait_ge(s_pg0, 4 * n)
                    dve.wait_ge(s_pv0, 4 * n)
                dve.wait_ge(s_rr, n + 1)
                nc.vector.tensor_tensor(view(xab, 0, [[260, 2], [1, PQ], [8, K0]]),
                                        view(mid, 128, [[0, 2], [K0, PQ], [1, K0]]),
                                        view(rr0, PQ, [[0, 2], [1, PQ], [0, K0]]), ALU.mult).then_inc(s_xab, 1)
                nc.vector.tensor_tensor(view(xab, 4, [[252, 2], [1, PQ], [8, K0]]),
                                        view(mid, 256, [[0, 2], [K0, PQ], [1, K0]]),
                                        view(rr0, 0, [[PQ, 2], [1, PQ], [0, K0]]), ALU.mult).then_inc(s_xab, 1)

            def mix_chunk(b, q, t):
                n = 4 * (NQ * b + q) + t
                if q:
                    dst = tq[:, t % 2]
                    if q > 1 or t > 1:
                        dve.wait_ge(s_tacc, 12 * b + 4 * (q - 1) + t - 1)
                    elif not is_zero(b):
                        dve.wait_ge(s_tacc, 12 * b)
                else:
                    dst = tacc[:, :, NO4 * t:NO4 * t + NO4, :]
                    if not is_zero(b) and t == 0:
                        dve.wait_ge(s_l1, b)
                        dve.wait_ge(s_cc, 4 * b)
                dve.wait_ge(s_xab, 2 * (NQ * b + q + 1))
                if q or t:
                    dve.wait_ge(s_red, 2 * n - 1)
                elif not is_zero(b):
                    dve.wait_ge(s_red1, 2 * U1 * b)
                pr = prod_v[:, :].rearrange("p (o n) -> p o n", o=NO4)
                nc.vector.tensor_tensor(pr, w0[:, NO4 * t:NO4 * t + NO4, q].rearrange("p o k s c -> p o (k s c)"),
                                        view(xab, 0, [[0, NO4], [1, 256]]), ALU.mult).then_inc(s_pv0, 1)
                dve.wait_ge(s_pv0, n + 1)
                nc.vector.tensor_reduce(dst[:, 0], prod_v[:, :].rearrange("p (o k n) -> p o k n", o=NO4, k=K0),
                                        AX.X, ALU.add).then_inc(s_red, 1)
                dve.wait_ge(s_pg0, n + 1)
                nc.vector.tensor_reduce(dst[:, 1],
                                        prod_g[:, t % 2, :].rearrange("p (o k n) -> p o k n", o=NO4, k=K0),
                                        AX.X, ALU.add).then_inc(s_red, 1)

            def cross_terms(a):
                dve.wait_ge(s_keep, 2 * NQ * (a + 1))
                dve.wait_ge(s_red, 8 * NQ * (a + 1))
                for r in range(2):
                    c = prod_v[:, 512 * r:512 * r + 512]
                    dve.wait_ge(s_ah, 2 * a + r + 1)
                    nc.vector.tensor_tensor(c, mid[:, :], xt[:, r].rearrange("p a k -> p (a k)"), ALU.add)\
                        .then_inc(s_cadd, 1)
                    dve.wait_ge(s_cadd, 2 * a + r + 1)
                    nc.vector.tensor_tensor(c, c, ah[:, r, :], ALU.mult).then_inc(s_cmul, 1)
                    dve.wait_ge(s_cmul, 2 * a + r + 1)
                    nc.vector.tensor_reduce(dq[:, r, :], c.rearrange("p (a k) -> p a k", k=K0), AX.X, ALU.add)\
                        .then_inc(s_cred, 1)

            def layer1_statistics(a):
                dve.wait_ge(s_tot, a + 1)
                nc.vector.scalar_tensor_tensor(st1[:, 0, :], mid[:, 0:NP], 1.0 / (GROUP * H * W), var0[:, :],
                                               ALU.mult, ALU.add).then_inc(s_st1, 1)
                nc.vector.tensor_scalar(st1[:, 1, :], mid[:, NP:2 * NP], 1.0 / GROUP, None, ALU.mult)\
                    .then_inc(s_st1, 1)
                dve.wait_ge(s_st1, 5 * a + 2)
                nc.vector.tensor_tensor(st1[:, 2, :], st1[:, 1, :], st1[:, 1, :], ALU.mult).then_inc(s_st1, 1)
                dve.wait_ge(s_st1, 5 * a + 3)
                nc.vector.tensor_tensor(st1[:, 3, :], st1[:, 0, :], st1[:, 2, :], ALU.subtract).then_inc(s_st1, 1)
                dve.wait_ge(s_st1, 5 * a + 4)
                nc.vector.tensor_scalar(st1[:, 0, :], st1[:, 3, :], 0.0, EPS, ALU.max, ALU.add).then_inc(s_st1, 1)
                dve.wait_ge(s_rs1, a + 1)
                nc.vector.tensor_scalar(rr1[:, 0, :], rr1[:, 1, :], -1.0, None, ALU.mult).then_inc(s_rr1, 1)

            def layer1_spectrum(a):
                dve.wait_ge(s_l1, a + 1)
                flat = xb[:, :, :, :].rearrange("p r a k -> p (r a k)")
                nc.vector.tensor_tensor(flat, flat, mid[:, 0:384], ALU.add).then_inc(s_x1s, 1)
                dve.wait_ge(s_x1s, a + 1)
                dve.wait_ge(s_rr1, a + 1)
                nc.vector.tensor_tensor(view(xab1, 0, [[576, 2], [K1, NP], [1, K1]]),
                                        view(xb, 0, [[0, 2], [K1, NP], [1, K1]]),
                                        view(rr1, NP, [[0, 2], [1, NP], [0, K1]]), ALU.mult).then_inc(s_xab1, 1)
                nc.vector.tensor_tensor(view(xab1, 192, [[192, 2], [K1, NP], [1, K1]]),
                                        view(xb, 192, [[0, 2], [K1, NP], [1, K1]]),
                                        view(rr1, 0, [[NP, 2], [1, NP], [0, K1]]), ALU.mult).then_inc(s_xab1, 1)
                dve.wait_ge(s_xab1, 2 * (a + 1))

            def layer1_mix(a):
                for t in range(U1):
                    n = U1 * a + t
                    if t:
                        dve.wait_ge(s_red1, 2 * n - 1)
                    else:
                        dve.wait_ge(s_cred, 2 * (a + 1))
                    pr = prod_v[:, 0:384 * NO2].rearrange("p (o n) -> p o n", o=NO2)
                    nc.vector.tensor_tensor(pr, w1[:, NO2 * t:NO2 * t + NO2].rearrange("p o s c k -> p o (s c k)"),
                                            view(xab1, 0, [[0, NO2], [1, 384]]), ALU.mult).then_inc(s_pv1, 1)
                    dve.wait_ge(s_pv1, n + 1)
                    nc.vector.tensor_reduce(vacc[:, 0, NO2 * t:NO2 * t + NO2, :],
                                            view(prod_v, 0, [[384, NO2], [1, K1], [K1, 32]]), AX.X, ALU.add)\
                        .then_inc(s_red1, 1)
                    dve.wait_ge(s_pg1, n + 1)
                    nc.vector.tensor_reduce(vacc[:, 1, NO2 * t:NO2 * t + NO2, :],
                                            view(prod_g, 1024 * (t % 2), [[384, NO2], [1, K1], [K1, 32]]),
                                            AX.X, ALU.add).then_inc(s_red1, 1)

            def add_inverse_input(a):
                for u in range(4):
                    o, r = u // 2, u % 2
                    dve.wait_ge(s_pv, 4 * a + u + 1)
                    if u == 0:
                        dve.wait_ge(s_ccc, 4 * (a + 1))
                    c = csb[:, :, o, r, 0:K1]
                    nc.vector.tensor_tensor(c, c, mid[:, 0:192].rearrange("p (a k) -> p a k", k=K1), ALU.add)\
                        .then_inc(s_cs, 1)

            def add_pair(a, k):
                for i in range(2):
                    m = 2 * k + i
                    dve.wait_ge(s_x2[m % 4], a * 128 + 16 * (m // 4 + 1))
                for j in range(NJ):
                    for i in range(2):
                        u = 8 * k + 2 * j + i
                        dve.wait_ge(s_y, a * 128 + u + 1)
                        xs = x2[:, (2 * k + i) % 4, W * j:W * j + W]
                        nc.vector.tensor_tensor(xs, yb[u % NY][:, :], xs, ALU.add).then_inc(s_add, 1)

            def body(b, first, last):
                a = b - 1
                for s in range(STEPS):
                    if first and s < 8:
                        to_staging(s)
                        if s == 7:
                            dve.wait_ge(s_w0[0], 64 * 16)
                            dve.wait_ge(s_w0[1], 64 * 16)
                    if not first:
                        if s == LAST_QUAD_STEP:
                            quad_statistics(a, NQ - 1)
                            for t in range(4):
                                mix_chunk(a, NQ - 1, t)
                        if s == CROSS_STEP:
                            cross_terms(a)
                        if s == CC_STEP:
                            layer1_statistics(a)
                        if s == L1_STEP:
                            layer1_spectrum(a)
                            layer1_mix(a)
                        if s == PV_STEP:
                            add_inverse_input(a)
                    if not last:
                        if s in QUAD_STEP:
                            quad_statistics(b, QUAD_STEP.index(s))
                        for q, t in quad_chunks(s):
                            mix_chunk(b, q, t)
                    if not first:
                        for k in pass2_pairs(s):
                            add_pair(a, k)

            body(0, True, False)
            dve.wait_ge(s_w1, 4 * 4 * HO * 16)
            body(1, False, False)
            with dve.Fori(2, B) as b:
                body(b, False, False)
            body(B, False, True)

        @block.gpsimd
        def _(pool):
            def inverse_std(b, q):
                n = NQ * b + q
                pool.wait_ge(s_st, 5 * (n + 1))
                if q or not is_zero(b):
                    pool.wait_ge(s_xab, 2 * n)
                nc.gpsimd.tensor_tensor(rr0[:, 1, :], st[:, 3, :], expo[:, 0:PQ], ALU.pow).then_inc(s_rs, 1)

            def mix_chunk(b, q, t):
                n = 4 * (NQ * b + q) + t
                pool.wait_ge(s_xab, 2 * (NQ * b + q + 1))
                if q or t > 1 or not is_zero(b):
                    pool.wait_ge(s_red, 2 * (n - 1))
                pr = prod_g[:, t % 2, :].rearrange("p (o n) -> p o n", o=NO4)
                nc.gpsimd.tensor_tensor(pr, w0[:, NO4 * t:NO4 * t + NO4, q].rearrange("p o k s c -> p o (k s c)"),
                                        view(xab, 256, [[0, NO4], [1, 256]]), ALU.mult).then_inc(s_pg0, 1)

            def accumulate(b, q, t):
                n = 4 * (NQ * b + q) + t
                pool.wait_ge(s_red, 2 * (n + 1))
                if q > 1:
                    pool.wait_ge(s_tacc, 12 * b + 4 * (q - 2) + t + 1)
                c = tacc[:, :, NO4 * t:NO4 * t + NO4, :]
                nc.gpsimd.tensor_tensor(c, c, tq[:, t % 2], ALU.add).then_inc(s_tacc, 1)

            def mix_chunks(b, chunks):
                chunks = list(chunks)
                for n, (q, t) in enumerate(chunks):
                    mix_chunk(b, q, t)
                    if n and chunks[n - 1][0]:
                        accumulate(b, *chunks[n - 1])
                if chunks and chunks[-1][0]:
                    accumulate(b, *chunks[-1])

            def layer1_std(a):
                pool.wait_ge(s_st1, 5 * (a + 1))
                pool.wait_ge(s_xab1, 2 * a)
                nc.gpsimd.tensor_tensor(rr1[:, 1, :], st1[:, 0, :], expo[:, :], ALU.pow).then_inc(s_rs1, 1)

            def layer1_mix(a):
                pool.wait_ge(s_xab1, 2 * (a + 1))
                for t in range(U1):
                    n = U1 * a + t
                    if t >= 2:
                        pool.wait_ge(s_red1, 2 * (n - 1))
                    else:
                        pool.wait_ge(s_red, 32 * (a + 1))
                    pr = prod_g[:, t % 2, 0:384 * NO2].rearrange("p (o n) -> p o n", o=NO2)
                    nc.gpsimd.tensor_tensor(pr, w1[:, NO2 * t:NO2 * t + NO2].rearrange("p o s c k -> p o (s c k)"),
                                            view(xab1, 384, [[0, NO2], [1, 384]]), ALU.mult).then_inc(s_pg1, 1)

            def body(b, first, last):
                a = b - 1
                for s in range(STEPS):
                    if not first:
                        if s == LAST_QUAD_STEP:
                            inverse_std(a, NQ - 1)
                            mix_chunks(a, [(NQ - 1, t) for t in range(4)])
                        if s == CC_STEP:
                            layer1_std(a)
                        if s == L1_STEP:
                            layer1_mix(a)
                    if not last:
                        if s in QUAD_STEP:
                            if s == QUAD_STEP[0] and not first:
                                pool.wait_ge(s_red1, 2 * U1 * b)
                            inverse_std(b, QUAD_STEP.index(s))
                        mix_chunks(b, quad_chunks(s))

            nc.gpsimd.memset(w1[:, :, :, :, :], 0.0).then_inc(s_zero, 1)
            nc.gpsimd.memset(prod_g[:, 0, 0:P], 0.0).then_inc(s_zero, 1)
            nc.gpsimd.memset(expo[:, :], -0.5).then_inc(s_zero, 1)
            pool.wait_ge(s_zero, 3)
            pool.wait_ge(s_w0[0], 64 * 16)
            pool.wait_ge(s_w0[1], 64 * 16)
            body(0, True, False)
            pool.wait_ge(s_w1, 4 * 4 * HO * 16)
            body(1, False, False)
            with pool.Fori(2, B) as b:
                body(b, False, False)
            body(B, False, True)


_INS = ["x", "L0_conv_coeff_real", "L0_conv_coeff_imag", "L0_conv_proj",
        "L1_conv_w1_real", "L1_conv_w1_imag", "L1_conv_w2_real", "L1_conv_w2_imag"]


def kernel(**inputs):
    import numpy as _np
    import concourse.bacc as _bacc
    from concourse import mybir as _mybir
    from concourse.bass_utils import run_bass_kernel_spmd as _run

    nc = _bacc.Bacc("TRN2", target_bir_lowering=False, num_devices=1, dynamic_dma_scratch_size=1024)
    arrays, args = {}, []
    for name, a in [(n, inputs[n]) for n in _INS] + [("table", constants())]:
        a = _np.ascontiguousarray(a)
        arrays[f"in_{name}_dram"] = a
        args.append(nc.dram_tensor(f"in_{name}_dram", a.shape, _mybir.dt.from_np(a.dtype), kind="ExternalInput").ap())
    args.append(nc.dram_tensor("out_0_dram", (B, C, H, W), _mybir.dt.float32, kind="ExternalOutput").ap())
    conv_preact_two_layers(nc, *args)
    r = _run(nc, [arrays], core_ids=[0])
    return r.results[0]["out_0_dram"]
```

```python
import math

import numpy as np

import concourse.bass as bass
from concourse import mybir
from contextlib import ExitStack

FP32 = mybir.dt.float32
BF16 = mybir.dt.bfloat16
ALU = mybir.AluOpType
ACT = mybir.ActivationFunctionType
AX = mybir.AxisListType

B, C, H, W = 8, 32, 512, 512
K0 = 32
K1 = 12
M1 = 2 * K1
P = 128
NJ = H // P
NW = W // P
NP = C // 2
NQ = 4
PQ = NP // NQ
HO = C // 2
GROUP = 2 * H * W
EPS = 1e-5

MATS = ["rc", "rs", "rcn", "dc", "ah", "ahr0", "ahi0", "rc1", "rs1", "rcn1", "s1", "s1r0", "s1i0",
        "qc0", "qc1", "qs0", "qs1", "qsn0", "qsn1", "pc0", "pc1", "ps0", "ps1", "psn0", "psn1", "ident"]
MAT_AT = {name: n * P for n, name in enumerate(MATS)}
SUMS = ["ones", "sums", "w8", "w4", "ysum"]
SUM_AT = {name: len(MATS) * P + n for n, name in enumerate(SUMS)}
ROW_DFT = len(MATS) * P + 8
COL_DFT = ROW_DFT + NJ * 2 * K0
ROW_INV = COL_DFT + NW * 2 * K0
COL_INV = ROW_INV + H
NCONST = COL_INV + 2 * W


def constants():
    t = np.zeros((P, NCONST), np.float64)

    def z(i, cs, k):
        return 64 * i + 32 * cs + k

    def g(o, i, k):
        return 64 * o + 32 * i + k

    def put(name, row, col, v):
        t[row, MAT_AT[name] + col] += v

    for i in range(2):
        for o in range(2):
            for k in range(K0):
                put("rc", z(i, 0, k), g(o, i, k), 1)
                put("rcn", z(i, 0, k), g(o, i, k), -1)
                put("rs", z(i, 1, k), g(o, i, k), -1)
            for i2 in range(2):
                put("dc", z(i2, 0, 0), g(o, i, 0), -0.5)
            for m in range(M1):
                j, sign = (m, -1) if m < K1 else (M1 - m, 1)
                put("rc1", z(i, 0, j), g(o, i, m), 1)
                put("rcn1", z(i, 0, j), g(o, i, m), -1)
                put("rs1", z(i, 1, j), g(o, i, m), sign)
    for o in range(2):
        for i in range(2):
            for rep in range(2):
                for k in range(K0):
                    put("ah", g(o, i, k), g(rep, o, k), 0.5)
                    put("ahr0", g(o, i, k), g(rep, o, k), 0.25 if k else 0.5)
                    put("ahi0", g(o, i, k), g(rep, o, k), 0.25 if k else 0)
                for m in range(K1):
                    put("s1", g(o, i, m), g(rep, o, m), 1)
                for m in range(1, K1):
                    put("s1r0", g(o, i, m), g(rep, o, m), 0.5)
                    put("s1i0", g(o, i, m), g(rep, o, m), 0.5)
                for m in range(K1, M1):
                    put("s1r0", g(o, i, M1 - m), g(rep, o, m), 0.5)
                    put("s1i0", g(o, i, M1 - m), g(rep, o, m), -0.5)
                for i2 in range(2):
                    put("s1r0", g(o, i, 0), g(rep, i2, 0), 0.5 if i2 == o else -0.5)
            for k in range(K0):
                put(f"qc{o}", g(o, i, k), k, 1)
                put(f"qs{o}", g(o, i, k), 64 + k, 1)
                put(f"qsn{o}", g(o, i, k), 64 + k, -1)
            for m in range(M1):
                r = m if m < K1 else K0 + m - K1
                put(f"pc{o}", g(o, i, m), r, 1)
                put(f"ps{o}", g(o, i, m), 64 + r, 1)
                put(f"psn{o}", g(o, i, m), 64 + r, -1)
    t[:, SUM_AT["ones"]] = 1
    t[:, MAT_AT["ident"]:MAT_AT["ident"] + P] = np.eye(P)
    for i in range(2):
        t[z(i, 0, 0), SUM_AT["sums"]] = 1
        t[g(0, i, 0), SUM_AT["w4"]] = -4
        t[g(0, i, 0), SUM_AT["ysum"]] = 2
    t[0:64, SUM_AT["w8"]] = 8

    def angle(a, b, n):
        return 2 * np.pi * np.mod(np.multiply.outer(a, b), n) / n

    part, kx = np.arange(P), np.arange(K0)
    for j in range(NJ):
        a = angle(NJ * part + j, kx, H)
        t[:, ROW_DFT + 64 * j:ROW_DFT + 64 * j + 64] = np.concatenate([np.cos(a), np.sin(a)], 1)
        a = angle(P * j + part, kx, W)
        t[:, COL_DFT + 64 * j:COL_DFT + 64 * j + 64] = np.concatenate([np.cos(a), np.sin(a)], 1)
        rows = np.concatenate([kx, np.arange(H - K1, H)])
        a = angle(rows, NJ * part + j, H)
        t[0:K0 + K1, ROW_INV + P * j:ROW_INV + P * j + P] = np.cos(a)
        t[64:64 + K0 + K1, ROW_INV + P * j:ROW_INV + P * j + P] = np.sin(a)
    gain = np.where(kx == 0, 1.0, 2.0)[:, None] / (H * W)
    a = angle(kx, np.arange(W), W)
    for i in range(2):
        t[64 * i:64 * i + 32, COL_INV + W * i:COL_INV + W * i + W] = gain * np.cos(a)
        t[64 * i + 32:64 * i + 64, COL_INV + W * i:COL_INV + W * i + W] = -gain * np.sin(a)
    return t.astype(np.float32)


STEPS = NP
INV_STEP = 8
LAG = INV_STEP + 1
QUAD_STEP = [9, 11, 13]
LAST_QUAD_STEP, CROSS_STEP, TOTAL_STEP = 1, 3, 4
QUAD_CHUNKS = {9: ((), (0,)), 10: ((1,), (2,)), 11: ((3,), (4,)), 12: ((5,), (6,)), 13: ((7,), (8,)),
               14: ((9,), (10,)), 15: ((11,), ())}
LAST_CHUNKS = {1: ((12,), (13,)), 2: ((14,), (15,))}
L1_UNITS = {5: ((0,), (1, 2)), 6: ((3,), (4, 5)), 7: ((6,), (7,))}
NO4 = 4
NO2 = 2
NY = 4
U1 = HO // NO2


def conv_preact_two_layers(nc, x, coeff_re, coeff_im, proj, w1_re, w1_im, w2_re, w2_im, table, out):
    xv = x.rearrange("b c (p j) w -> b c p (j w)", j=NJ)
    ov = out.rearrange("b c (p j) w -> b c p (j w)", j=NJ)

    ctx = ExitStack()
    with ctx:
        def sb(name, shape, dt=FP32):
            return ctx.enter_context(nc.sbuf_tensor(name, shape, dt))

        def sem(name):
            return ctx.enter_context(nc.semaphore(name))

        def view(t, offset, dims, parts=P, part0=0):
            row = t[:].ap[0][0]
            return bass.AP(tensor=t[:].tensor, offset=part0 * row + offset, ap=[[row, parts], *dims])

        const = sb("const", [P, NCONST])
        w0 = sb("w0", [P, HO, NQ, K0, 2, PQ])
        w1 = sb("w1", [P, HO, 2, NP, K1])
        x1 = sb("x1", [P, 4, NJ * W])
        x2 = sb("x2", [P, 4, NJ * W])
        rows = sb("rows", [P, W])
        cols = sb("cols", [P, NW, P])
        zq = sb("zq", [P, 2 * PQ, 2, K0])
        xt = sb("xt", [P, 2, NP, K0])
        xb = sb("xb", [P, 2, NP, K1])
        junk = sb("junk", [P, 1024], BF16)
        sq = sb("sq", [P, NP, 4])
        prod_v = sb("prod_v", [P, 1024])
        prod_g = sb("prod_g", [P, 2, 1024])
        tacc = sb("tacc", [P, 2, HO, K0])
        tq = sb("tq", [P, 2, 2, NO4, K0])
        xab = sb("xab", [P, 2, K0, 2, PQ])
        xab1 = sb("xab1", [P, 2, 2, NP, K1])
        vacc = tq[:, :, :, :, :].rearrange("p a b o k -> p (a b o k)")[:, 0:2 * HO * K1]\
            .rearrange("p (r o k) -> p r o k", r=2, k=K1)
        csb = sb("csb", [P, NP, 2, 2, K0])
        gsb = sb("gsb", [P, 2, H])
        st = sb("st", [P, 5, PQ])
        var0 = sb("var0", [P, NP])
        rr0 = sb("rr0", [P, 2, PQ])
        st1 = sb("st1", [P, 4, NP])
        rr1 = sb("rr1", [P, 2, NP])
        dq = sb("dq", [P, 2, NP])
        expo = sb("expo", [P, NP])
        ah = prod_g[:, 0, :].rearrange("p (r n) -> p r n", r=2)

        def bank(name):
            return ctx.enter_context(nc.psum_tensor(name, [P, 512], FP32))

        fa = bank("fa")
        ft = bank("ft")
        zb = bank("zb")
        mid = bank("mid")
        yb = [bank(f"y{n}") for n in range(NY)]

        def mat(name):
            return const[:, MAT_AT[name]:MAT_AT[name] + P]

        def total(name):
            return const[:, SUM_AT[name]:SUM_AT[name] + 1].broadcast_to([P, P])

        row_dft = const[:, ROW_DFT:COL_DFT].rearrange("p (j n) -> p j n", j=NJ)
        col_dft = const[:, COL_DFT:ROW_INV].rearrange("p (j n) -> p j n", j=NW)
        row_inv = const[:, ROW_INV:COL_INV]
        col_inv = const[:, COL_INV:NCONST].rearrange("p (i w) -> p i w", i=2)

        coef = [x2[:, n, :].rearrange("p (r n) -> p r n", r=2) for n in (0, 1)]
        wst = [x2[:, n, :].rearrange("p (i q k s c) -> p i q k s c", i=2, q=NQ, k=K0, s=2) for n in (2, 3)]
        projb = prod_g[:, 0, 0:P]

        s_const = sem("s_const")
        s_zero = sem("s_zero")
        s_proj = sem("s_proj")
        s_w1 = sem("s_w1")
        s_coef = [sem("s_coef0"), sem("s_coef1")]
        s_wc = sem("s_wc")
        s_wst = sem("s_wst")
        s_w0 = [sem("s_w0a"), sem("s_w0b")]
        s_x1 = [sem(f"s_x1_{n}") for n in range(4)]
        s_x2 = [sem(f"s_x2_{n}") for n in range(4)]
        s_out = [sem(f"s_out_{n}") for n in range(4)]
        s_fa = sem("s_fa")
        s_sq = sem("s_sq")
        s_junk = sem("s_junk")
        s_rows = sem("s_rows")
        s_ft = sem("s_ft")
        s_cols = sem("s_cols")
        s_zb = sem("s_zb")
        s_zq = sem("s_zq")
        s_quad = sem("s_quad")
        s_keep = sem("s_keep")
        s_st = sem("s_st")
        s_rs = sem("s_rs")
        s_rr = sem("s_rr")
        s_xab = sem("s_xab")
        s_pv0 = sem("s_pv0")
        s_pg0 = sem("s_pg0")
        s_red = sem("s_red")
        s_tacc = sem("s_tacc")
        s_cross = sem("s_cross")
        s_ah = sem("s_ah")
        s_cadd = sem("s_cadd")
        s_cmul = sem("s_cmul")
        s_cred = sem("s_cred")
        s_tot = sem("s_tot")
        s_st1 = sem("s_st1")
        s_rs1 = sem("s_rs1")
        s_rr1 = sem("s_rr1")
        s_cc = sem("s_cc")
        s_ccc = sem("s_ccc")
        s_l1 = sem("s_l1")
        s_x1s = sem("s_x1s")
        s_xab1 = sem("s_xab1")
        s_pv1 = sem("s_pv1")
        s_pg1 = sem("s_pg1")
        s_red1 = sem("s_red1")
        s_gp = sem("s_gp")
        s_gs = sem("s_gs")
        s_y = sem("s_y")
        s_add = sem("s_add")

        block = ctx.enter_context(nc.Block())

        def is_zero(b):
            return isinstance(b, int) and b == 0

        def is_one(b):
            return isinstance(b, int) and b == 1

        def pass2_pairs(b, s):
            if is_zero(b) or is_one(b) and s < LAG:
                return []
            if s < LAG:
                return [(b - 2, NP - LAG + s)]
            if isinstance(b, int) and b == B:
                return [(b - 1, k) for k in range(NP)] if s == LAG else []
            return [(b - 1, s - LAG)]

        def quad_chunks(s, table=QUAD_CHUNKS):
            return [[(n // 4, n % 4) for n in part] for part in table.get(s, ((), ()))]

        @block.sync
        def _(sp):
            def load_pass1(b, s):
                if s >= 2 or not is_zero(b):
                    sp.wait_ge(s_fa, b * NP + s - 1)
                    sp.wait_ge(s_sq, b * NP + s - 1)
                for i in range(2):
                    m = 2 * s + i
                    sp.dma_start(x1[:, m % 4, :], xv[b, m]).then_inc(s_x1[m % 4], 16)

            def load_pass2(a, k):
                if is_zero(a) and k == 0:
                    sp.wait_ge(s_w0[0], 64 * 16)
                    sp.wait_ge(s_w0[1], 64 * 16)
                for i in range(2):
                    m = 2 * k + i
                    n = m % 4
                    if m >= 4 or not is_zero(a):
                        sp.wait_ge(s_out[n], a * 128 + 16 * (m // 4))
                    sp.dma_start(x2[:, n, :], xv[a, m]).then_inc(s_x2[n], 16)

            def load_w1(first, count):
                for d in range(first, first + count):
                    n, o, i, ho = d // 64, d // 32 % 2, d // 16 % 2, d % 16
                    src = (w1_re, w1_im, w2_re, w2_im)[n]
                    part = 64 * o + 32 * i + K1 * (n // 2)
                    sp.dma_start(w1[part:part + K1, ho, n % 2], src[i::2, 2 * ho + o].rearrange("c x y -> x c y"),
                                 allow_slow_non_contiguous=True).then_inc(s_w1, 16)

            sp.dma_start(const[:, :], table).then_inc(s_const, 16)

            def load_coef(k):
                n = k % 2
                if k >= 2:
                    sp.wait_ge(s_wc, 4 * (k - 1))
                for r, src in enumerate((coeff_re, coeff_im)):
                    for kg in range(4):
                        sp.dma_start(coef[n][32 * kg:32 * kg + 32, r, :],
                                     src[:, 8 * kg + k].rearrange("r j c -> r (j c)")).then_inc(s_coef[n], 16)

            def scatter_w0(k):
                sp.wait_ge(s_wst, 8 * (k + 1))
                for kg in range(4):
                    for o in range(2):
                        for i in range(2):
                            part = 64 * o + 32 * i + 8 * kg + k
                            src = wst[k % 2][32 * kg + o:32 * kg + 32:2, i].rearrange("p q k s c -> p (q k s c)")
                            dst = w0[part:part + 1].rearrange("p o q k s c -> p o (q k s c)")
                            sp.dma_start(dst, src).then_inc(s_w0[k % 2], 16)

            def body(b):
                last = isinstance(b, int) and b == B - 1
                for s in range(STEPS):
                    if s + 1 < STEPS:
                        load_pass1(b, s + 1)
                    elif not last:
                        load_pass1(b + 1, 0)
                    if is_one(b) and s < 4:
                        load_w1(192 + 16 * s, 16)
                    for a, k in pass2_pairs(b, s):
                        load_pass2(a, k)

            load_pass1(0, 0)
            load_coef(0)
            load_coef(1)
            for s in range(STEPS):
                if s + 1 < STEPS:
                    load_pass1(0, s + 1)
                else:
                    load_pass1(1, 0)
                if s < 8:
                    scatter_w0(s)
                    if s + 2 < 8:
                        load_coef(s + 2)
                    if s == 0:
                        sp.wait_ge(s_zero, 3)
                    load_w1(4 * s, 4)
                else:
                    load_w1(32 + 20 * (s - 8), 20)
            body(1)
            with sp.Fori(2, B - 1) as b:
                body(b)
            body(B - 1)
            for s in range(STEPS):
                for a, k in pass2_pairs(B, s):
                    load_pass2(a, k)

        @block.tensor
        def _(pe):
            def wc_products(k):
                pe.wait_ge(s_coef[k % 2], 8 * 16 * (k // 2 + 1))
                for r in range(2):
                    for hh in range(2):
                        u = 4 * k + 2 * r + hh
                        if u >= NY:
                            pe.wait_ge(s_wst, 2 * (u - NY + 1))
                        nc.tensor.matmul(yb[u % NY][:, :], projb, coef[k % 2][:, r, 512 * hh:512 * hh + 512],
                                         start=True, stop=True).then_inc(s_wc, 1)

            def transposes(b, s):
                pe.wait_ge(s_rows, b * NP + s + 1)
                if s > 0 or not is_zero(b):
                    pe.wait_ge(s_cols, b * NP + s)
                for w in range(NW):
                    last = nc.tensor.transpose(ft[:, P * w:P * w + P], rows[:, P * w:P * w + P], mat("ident"))
                last.then_inc(s_ft, 1)

            def row_transform(b, s):
                if s or not is_zero(b):
                    pe.wait_ge(s_rows, b * NP + s)
                for i in range(2):
                    m = 2 * s + i
                    pe.wait_ge(s_x1[m % 4], b * 128 + 16 * (m // 4 + 1))
                for j in range(NJ):
                    for i in range(2):
                        last = nc.tensor.matmul(fa[64 * i:64 * i + 64, :], row_dft[:, j, :],
                                                x1[:, (2 * s + i) % 4, W * j:W * j + W],
                                                start=(j == 0), stop=(j == NJ - 1))
                last.then_inc(s_fa, 1)

            def col_transform(b, s):
                pe.wait_ge(s_cols, b * NP + s + 1)
                if s or not is_zero(b):
                    pe.wait_ge(s_zq, b * NP + s)
                for w in range(NW):
                    last = nc.tensor.matmul(zb[:, 0:2 * K0], cols[:, w, :], col_dft[:, w, :],
                                            start=(w == 0), stop=(w == NW - 1))
                last.then_inc(s_zb, 1)

            def quad_spectra(b, q):
                pe.wait_ge(s_zq, b * NP + PQ * (q + 1))
                pe.wait_ge(s_sq, b * NP + PQ * (q + 1))
                if q == 0 and not is_zero(b):
                    pe.wait_ge(s_ccc, 4 * b)
                if q:
                    pe.wait_ge(s_keep, 2 * (NQ * b + q))
                    pe.wait_ge(s_xab, 2 * (NQ * b + q))
                z = zq[:, PQ * (q % 2):PQ * (q % 2) + PQ]
                nc.tensor.matmul(mid[:, 0:16], total("ones"), sq[:, PQ * q:PQ * q + PQ, :], start=True, stop=True)
                nc.tensor.matmul(mid[:, 16:20], total("sums"), z[:, :, 0, 0], start=True, stop=True)
                for at, n, c, sn, cn in ((128, K0, "rc", "rs", "rcn"), (384, K1, "rc1", "rs1", "rcn1")):
                    re = mid[:, at:at + PQ * n]
                    im = mid[:, at + PQ * n:at + 2 * PQ * n]
                    nc.tensor.matmul(re, mat(c), z[:, :, 0, 0:n], start=True, stop=False)
                    nc.tensor.matmul(re, mat(sn), z[:, :, 1, 0:n], start=False, stop=False)
                    nc.tensor.matmul(re.rearrange("p (a k) -> p a k", k=n)[:, :, 0], mat("dc"), z[:, :, 0, 0],
                                     start=False, stop=True)
                    nc.tensor.matmul(im, mat(sn), z[:, :, 0, 0:n], start=True, stop=False)
                    last = nc.tensor.matmul(im, mat(cn), z[:, :, 1, 0:n], start=False, stop=True)
                last.then_inc(s_quad, 1)

            def cross_spectra(a, r):
                if r:
                    pe.wait_ge(s_ah, 2 * a + 1)
                    pe.wait_ge(s_cadd, 2 * a + 1)
                else:
                    pe.wait_ge(s_keep, 2 * NQ * (a + 1))
                    pe.wait_ge(s_xab, 2 * NQ * (a + 1))
                    pe.wait_ge(s_red, 32 * (a + 1))
                    pe.wait_ge(s_tacc, 12 * (a + 1))
                m3 = mid[:, :].rearrange("p (a k) -> p a k", k=K0)
                nc.tensor.matmul(m3[:, :, 1:K0], mat("ah"), tacc[:, r, :, 1:K0], start=True, stop=True)
                nc.tensor.matmul(m3[:, :, 0], mat("ahi0" if r else "ahr0"), tacc[:, r, :, 0], start=True, stop=True)\
                    .then_inc(s_cross, 1)

            def cross_totals(a):
                pe.wait_ge(s_cred, 2 * (a + 1))
                pe.wait_ge(s_ah, 2 * (a + 1))
                nc.tensor.matmul(mid[:, 0:NP], total("w8"), dq[:, 0, :], start=True, stop=False)
                nc.tensor.matmul(mid[:, 0:NP], total("w8"), dq[:, 1, :], start=False, stop=False)
                p0 = prod_v[:, 0:512].rearrange("p (a k) -> p a k", k=K0)
                nc.tensor.matmul(mid[:, 0:NP], total("w4"), p0[:, :, 0], start=False, stop=True)
                a0 = ah[:, 0, :].rearrange("p (a k) -> p a k", k=K0)
                nc.tensor.matmul(mid[:, NP:2 * NP], total("ysum"), a0[:, :, 0], start=True, stop=True)\
                    .then_inc(s_tot, 1)

            def layer1_input(a):
                pe.wait_ge(s_st1, 5 * a + 2)
                for r, col0 in enumerate(("s1r0", "s1i0")):
                    m3 = mid[:, 192 * r:192 * r + 192].rearrange("p (a k) -> p a k", k=K1)
                    nc.tensor.matmul(m3[:, :, 1:K1], mat("s1"), tacc[:, r, :, 1:K1], start=True, stop=True)
                    last = nc.tensor.matmul(m3[:, :, 0], mat(col0), tacc[:, r, :, 0], start=True, stop=True)
                last.then_inc(s_l1, 1)

            def inverse_input(a, u):
                o, r = u // 2, u % 2
                if u:
                    pe.wait_ge(s_ccc, 4 * a + u)
                else:
                    pe.wait_ge(s_x1s, a + 1)
                    pe.wait_ge(s_red1, 2 * U1 * (a + 1))
                m3 = mid[:, :].rearrange("p (a k) -> p a k", k=K0)[:, :, 0:K1]
                q_turn, p_turn = ("qs", "ps") if r else ("qsn", "psn")
                nc.tensor.matmul(mid[:, :], mat(f"qc{o}"), tacc[:, r], start=True, stop=False)
                nc.tensor.matmul(mid[:, :], mat(f"{q_turn}{o}"), tacc[:, 1 - r], start=False, stop=False)
                nc.tensor.matmul(m3, mat(f"pc{o}"), vacc[:, r], start=False, stop=False)
                nc.tensor.matmul(m3, mat(f"{p_turn}{o}"), vacc[:, 1 - r], start=False, stop=True).then_inc(s_cc, 1)

            def inverse_rows(a, k, transposed):
                if k == 0:
                    pe.wait_ge(s_ccc, 4 * (a + 1))
                if k or not is_zero(a):
                    pe.wait_ge(s_gs, a * NP + k)
                pe.wait_ge(s_cols, transposed)
                nc.tensor.matmul(ft[:, :], csb[:, k].rearrange("p i r k -> p (i r k)"), row_inv,
                                 start=True, stop=True).then_inc(s_gp, 1)

            def inverse_cols(a, k, i):
                if i == 0:
                    pe.wait_ge(s_gs, a * NP + k + 1)
                for j in range(NJ):
                    u = 8 * k + 4 * i + j
                    if u >= NY or not is_zero(a):
                        pe.wait_ge(s_add, a * 128 + max(u - NY + 1, 0))
                    nc.tensor.matmul(yb[u % NY][:, :], gsb[:, k % 2, P * j:P * j + P],
                                     col_inv[:, i, :], start=True, stop=True).then_inc(s_y, 1)

            def body(b, first, last):
                a = b - 1
                for s in range(STEPS):
                    earlier = (s or not first) and not (last and s)
                    pairs = pass2_pairs(b, s)
                    if pairs:
                        inverse_rows(*pairs[0], b * NP if last and s else b * NP + s - 1)
                    if not last:
                        row_transform(b, s)
                    if not first:
                        if s == LAST_QUAD_STEP:
                            quad_spectra(a, NQ - 1)
                        if s == CROSS_STEP:
                            cross_spectra(a, 0)
                        if s == TOTAL_STEP:
                            cross_totals(a)
                        if s == INV_STEP:
                            inverse_input(a, 0)
                    if not last and s in QUAD_STEP:
                        quad_spectra(b, QUAD_STEP.index(s))
                    if pairs:
                        inverse_cols(*pairs[0], 0)
                    if earlier:
                        transposes(b, s - 1)
                    if not first:
                        if s == CROSS_STEP:
                            cross_spectra(a, 1)
                        if s == TOTAL_STEP:
                            layer1_input(a)
                        if s == INV_STEP:
                            inverse_input(a, 1)
                    for n, (a2, k) in enumerate(pairs):
                        if n:
                            inverse_cols(a2, k, 0)
                        if n + 1 < len(pairs):
                            inverse_rows(*pairs[n + 1], b * NP)
                        inverse_cols(a2, k, 1)
                    if not first and s == INV_STEP:
                        inverse_input(a, 2)
                    if earlier:
                        col_transform(b, s - 1)
                    if first and s < 8:
                        if s == 0:
                            pe.wait_ge(s_proj, 4 * 16)
                        wc_products(s)
                    if not first and s == INV_STEP:
                        inverse_input(a, 3)
            pe.wait_ge(s_const, 16)
            body(0, True, False)
            body(1, False, False)
            with pe.Fori(2, B) as b:
                body(b, False, False)
            body(B, False, True)

        @block.scalar
        def _(act):
            def copy(dst, src):
                return nc.scalar.activation(dst, src, ACT.Copy)

            def squares(b, s):
                for i in range(2):
                    m = 2 * s + i
                    act.wait_ge(s_x1[m % 4], b * 128 + 16 * (m // 4 + 1))
                    if i == 0 and not is_zero(b):
                        act.wait_ge(s_quad, NQ * (b - 1) + s // PQ + 1)
                    for hh in range(2):
                        if i or hh:
                            act.wait_ge(s_junk, 3 * NP * b + 3 * s + 2 * i + hh)
                        elif s or not is_zero(b):
                            act.wait_ge(s_sq, NP * b + s)
                        last = nc.scalar.activation(junk[:, :], x1[:, m % 4, 1024 * hh:1024 * hh + 1024], ACT.Square,
                                                    accum_out=sq[:, s, 2 * i + hh:2 * i + hh + 1])
                        if i == 0 or hh == 0:
                            last.then_inc(s_junk, 1)
                last.then_inc(s_sq, 1)

            def copy_rows(b, s):
                act.wait_ge(s_fa, b * NP + s + 1)
                if s or not is_zero(b):
                    act.wait_ge(s_ft, b * NP + s)
                copy(rows[:, :], fa[:, :]).then_inc(s_rows, 1)

            def copy_cols(b, s):
                act.wait_ge(s_ft, b * NP + s + 1)
                if s or not is_zero(b):
                    act.wait_ge(s_zb, b * NP + s)
                copy(cols[:, :, :].rearrange("p a b -> p (a b)"), ft[:, :]).then_inc(s_cols, 1)

            def copy_spectrum(b, s):
                act.wait_ge(s_zb, b * NP + s + 1)
                if s >= 8 or not is_zero(b):
                    act.wait_ge(s_quad, NQ * b + (s - 8) // PQ + 1)
                copy(zq[:, s % (2 * PQ)].rearrange("p t k -> p (t k)"), zb[:, 0:2 * K0]).then_inc(s_zq, 1)

            def keep_quad(b, q):
                act.wait_ge(s_quad, NQ * b + q + 1)
                if q == 0 and not is_zero(b):
                    act.wait_ge(s_xab1, 2 * b)
                for dst, at, n in ((xt, 128, K0), (xb, 384, K1)):
                    copy(dst[:, :, PQ * q:PQ * q + PQ, :],
                         mid[:, at:at + 2 * PQ * n].rearrange("p (r a k) -> p r a k", r=2, k=n)).then_inc(s_keep, 1)

            def copy_cross(a, r):
                act.wait_ge(s_cross, 2 * a + r + 1)
                copy(ah[:, r, :], mid[:, :]).then_inc(s_ah, 1)

            def copy_inverse_input(a, u):
                o, r = u // 2, u % 2
                if u == 0:
                    act.wait_ge(s_gp, NP * a)
                act.wait_ge(s_cc, 4 * a + u + 1)
                copy(csb[:, :, o, r, :], mid[:, :].rearrange("p (a k) -> p a k", k=K0)).then_inc(s_ccc, 1)

            def copy_inverse_rows(a, k):
                act.wait_ge(s_gp, a * NP + k + 1)
                act.wait_ge(s_y, a * 128 + 8 * max(k - 1, 0))
                copy(gsb[:, k % 2, :], ft[:, :]).then_inc(s_gs, 1)

            def store(a, k, i):
                m = 2 * k + i
                act.wait_ge(s_add, a * 128 + 4 * (m + 1))
                act.dma_start(ov[a, m], x2[:, m % 4, :]).then_inc(s_out[m % 4], 16)

            def body(b, first, last):
                a = b - 1
                for s in range(STEPS):
                    earlier = (s or not first) and not (last and s)
                    pairs = pass2_pairs(b, s)
                    if pairs:
                        copy_inverse_rows(*pairs[0])
                    if not last:
                        squares(b, s)
                    if not first:
                        if s == LAST_QUAD_STEP:
                            keep_quad(a, NQ - 1)
                        if s == CROSS_STEP:
                            copy_cross(a, 0)
                        if s == INV_STEP:
                            copy_inverse_input(a, 0)
                    if not last and s in QUAD_STEP:
                        keep_quad(b, QUAD_STEP.index(s))
                    if earlier:
                        copy_cols(b, s - 1)
                    if not last:
                        copy_rows(b, s)
                    if not first:
                        if s == CROSS_STEP:
                            copy_cross(a, 1)
                        if s == INV_STEP:
                            copy_inverse_input(a, 1)
                            copy_inverse_input(a, 2)
                    if earlier:
                        copy_spectrum(b, s - 1)
                    if not first and s == INV_STEP:
                        copy_inverse_input(a, 3)
                    for n, (a2, k) in enumerate(pairs):
                        if n + 1 < len(pairs):
                            store(a2, k, 0)
                            copy_inverse_rows(*pairs[n + 1])
                            store(a2, k, 1)
                        else:
                            store(a2, k, 0)
                            store(a2, k, 1)

            act.wait_ge(s_zero, 2)
            for kg in range(4):
                act.dma_start(prod_g[32 * kg:32 * kg + 32, 0, 32 * kg:32 * kg + 32],
                              proj.rearrange("o r -> r o"), allow_slow_non_contiguous=True).then_inc(s_proj, 16)
            body(0, True, False)
            body(1, False, False)
            with act.Fori(2, B) as b:
                body(b, False, False)
            body(B, False, True)
            for n in range(4):
                act.wait_ge(s_out[n], 16 * B * C // 4)

        @block.vector
        def _(dve):
            def to_staging(k):
                if k >= 2:
                    dve.wait_ge(s_w0[k % 2], 16 * 16 * (k // 2))
                for r in range(2):
                    for hh in range(2):
                        u = 4 * k + 2 * r + hh
                        dve.wait_ge(s_wc, u + 1)
                        for i in range(2):
                            src = yb[u % NY][:, :].rearrange("p (k q c i) -> p i q k c", q=NQ, c=PQ, i=2)[:, i]
                            dst = wst[k % 2][:, i, :, 16 * hh:16 * hh + 16, r, :]
                            nc.vector.tensor_copy(dst, src).then_inc(s_wst, 1)

            def quad_statistics(b, q):
                n = NQ * b + q
                dve.wait_ge(s_keep, 2 * (n + 1))
                nc.vector.tensor_reduce(st[:, 0, :], mid[:, 0:16].rearrange("p (a n) -> p a n", n=4), AX.X, ALU.add)\
                    .then_inc(s_st, 1)
                nc.vector.tensor_scalar(st[:, 1, :], mid[:, 16:20], 1.0 / GROUP, None, ALU.mult).then_inc(s_st, 1)
                dve.wait_ge(s_st, 5 * n + 2)
                nc.vector.tensor_tensor(st[:, 2, :], st[:, 1, :], st[:, 1, :], ALU.mult).then_inc(s_st, 1)
                dve.wait_ge(s_st, 5 * n + 3)
                v = var0[:, PQ * q:PQ * q + PQ]
                nc.vector.scalar_tensor_tensor(v, st[:, 0, :], 1.0 / GROUP, st[:, 2, :], ALU.mult, ALU.subtract)\
                    .then_inc(s_st, 1)
                dve.wait_ge(s_st, 5 * n + 4)
                nc.vector.tensor_scalar(st[:, 3, :], v, 0.0, EPS, ALU.max, ALU.add).then_inc(s_st, 1)
                dve.wait_ge(s_rs, n + 1)
                nc.vector.tensor_scalar(rr0[:, 0, :], rr0[:, 1, :], -1.0, None, ALU.mult).then_inc(s_rr, 1)
                if q or not is_zero(b):
                    dve.wait_ge(s_pg0, 4 * n)
                    dve.wait_ge(s_pv0, 4 * n)
                dve.wait_ge(s_rr, n + 1)
                nc.vector.tensor_tensor(view(xab, 0, [[260, 2], [1, PQ], [8, K0]]),
                                        view(mid, 128, [[0, 2], [K0, PQ], [1, K0]]),
                                        view(rr0, PQ, [[0, 2], [1, PQ], [0, K0]]), ALU.mult).then_inc(s_xab, 1)
                nc.vector.tensor_tensor(view(xab, 4, [[252, 2], [1, PQ], [8, K0]]),
                                        view(mid, 256, [[0, 2], [K0, PQ], [1, K0]]),
                                        view(rr0, 0, [[PQ, 2], [1, PQ], [0, K0]]), ALU.mult).then_inc(s_xab, 1)

            def mix_chunk(b, q, t):
                n = 4 * (NQ * b + q) + t
                if q:
                    dst = tq[:, t % 2]
                    if q > 1 or t > 1:
                        dve.wait_ge(s_tacc, 12 * b + 4 * (q - 1) + t - 1)
                    elif not is_zero(b):
                        dve.wait_ge(s_tacc, 12 * b)
                else:
                    dst = tacc[:, :, NO4 * t:NO4 * t + NO4, :]
                    if not is_zero(b) and t == 0:
                        dve.wait_ge(s_cc, 4 * b)
                dve.wait_ge(s_xab, 2 * (NQ * b + q + 1))
                if q or t:
                    dve.wait_ge(s_red, 2 * n - 1)
                elif not is_zero(b):
                    dve.wait_ge(s_red1, 2 * U1 * b)
                pr = prod_v[:, :].rearrange("p (o n) -> p o n", o=NO4)
                nc.vector.tensor_tensor(pr, w0[:, NO4 * t:NO4 * t + NO4, q].rearrange("p o k s c -> p o (k s c)"),
                                        view(xab, 0, [[0, NO4], [1, 256]]), ALU.mult).then_inc(s_pv0, 1)
                dve.wait_ge(s_pv0, n + 1)
                nc.vector.tensor_reduce(dst[:, 0], prod_v[:, :].rearrange("p (o k n) -> p o k n", o=NO4, k=K0),
                                        AX.X, ALU.add).then_inc(s_red, 1)
                dve.wait_ge(s_pg0, n + 1)
                nc.vector.tensor_reduce(dst[:, 1],
                                        prod_g[:, t % 2, :].rearrange("p (o k n) -> p o k n", o=NO4, k=K0),
                                        AX.X, ALU.add).then_inc(s_red, 1)

            def cross_terms(a, r):
                if r == 0:
                    dve.wait_ge(s_keep, 2 * NQ * (a + 1))
                    dve.wait_ge(s_red, 8 * NQ * (a + 1))
                c = prod_v[:, 512 * r:512 * r + 512]
                dve.wait_ge(s_ah, 2 * a + r + 1)
                nc.vector.tensor_tensor(c, mid[:, :], xt[:, r].rearrange("p a k -> p (a k)"), ALU.add)\
                    .then_inc(s_cadd, 1)
                dve.wait_ge(s_cadd, 2 * a + r + 1)
                nc.vector.tensor_tensor(c, c, ah[:, r, :], ALU.mult).then_inc(s_cmul, 1)
                dve.wait_ge(s_cmul, 2 * a + r + 1)
                nc.vector.tensor_reduce(dq[:, r, :], c.rearrange("p (a k) -> p a k", k=K0), AX.X, ALU.add)\
                    .then_inc(s_cred, 1)

            def layer1_statistics(a):
                dve.wait_ge(s_tot, a + 1)
                nc.vector.scalar_tensor_tensor(st1[:, 0, :], mid[:, 0:NP], 1.0 / (GROUP * H * W), var0[:, :],
                                               ALU.mult, ALU.add).then_inc(s_st1, 1)
                nc.vector.tensor_scalar(st1[:, 1, :], mid[:, NP:2 * NP], 1.0 / GROUP, None, ALU.mult)\
                    .then_inc(s_st1, 1)
                dve.wait_ge(s_st1, 5 * a + 2)
                nc.vector.tensor_tensor(st1[:, 2, :], st1[:, 1, :], st1[:, 1, :], ALU.mult).then_inc(s_st1, 1)
                dve.wait_ge(s_st1, 5 * a + 3)
                nc.vector.tensor_tensor(st1[:, 3, :], st1[:, 0, :], st1[:, 2, :], ALU.subtract).then_inc(s_st1, 1)
                dve.wait_ge(s_st1, 5 * a + 4)
                nc.vector.tensor_scalar(st1[:, 0, :], st1[:, 3, :], 0.0, EPS, ALU.max, ALU.add).then_inc(s_st1, 1)
                dve.wait_ge(s_rs1, a + 1)
                nc.vector.tensor_scalar(rr1[:, 0, :], rr1[:, 1, :], -1.0, None, ALU.mult).then_inc(s_rr1, 1)

            def layer1_spectrum(a):
                dve.wait_ge(s_l1, a + 1)
                flat = xb[:, :, :, :].rearrange("p r a k -> p (r a k)")
                nc.vector.tensor_tensor(flat, flat, mid[:, 0:384], ALU.add).then_inc(s_x1s, 1)
                dve.wait_ge(s_x1s, a + 1)
                dve.wait_ge(s_rr1, a + 1)
                nc.vector.tensor_tensor(view(xab1, 0, [[576, 2], [K1, NP], [1, K1]]),
                                        view(xb, 0, [[0, 2], [K1, NP], [1, K1]]),
                                        view(rr1, NP, [[0, 2], [1, NP], [0, K1]]), ALU.mult).then_inc(s_xab1, 1)
                nc.vector.tensor_tensor(view(xab1, 192, [[192, 2], [K1, NP], [1, K1]]),
                                        view(xb, 192, [[0, 2], [K1, NP], [1, K1]]),
                                        view(rr1, 0, [[NP, 2], [1, NP], [0, K1]]), ALU.mult).then_inc(s_xab1, 1)

            def layer1_mix(a, units):
                for t in units:
                    n = U1 * a + t
                    if t:
                        dve.wait_ge(s_red1, 2 * n - 1)
                    else:
                        dve.wait_ge(s_cred, 2 * (a + 1))
                        dve.wait_ge(s_xab1, 2 * (a + 1))
                        if is_zero(a):
                            dve.wait_ge(s_w1, 4 * 4 * HO * 16)
                    pr = prod_v[:, 0:384 * NO2].rearrange("p (o n) -> p o n", o=NO2)
                    nc.vector.tensor_tensor(pr, w1[:, NO2 * t:NO2 * t + NO2].rearrange("p o s c k -> p o (s c k)"),
                                            view(xab1, 0, [[0, NO2], [1, 384]]), ALU.mult).then_inc(s_pv1, 1)
                    dve.wait_ge(s_pv1, n + 1)
                    nc.vector.tensor_reduce(vacc[:, 0, NO2 * t:NO2 * t + NO2, :],
                                            view(prod_v, 0, [[384, NO2], [1, K1], [K1, 32]]), AX.X, ALU.add)\
                        .then_inc(s_red1, 1)
                    dve.wait_ge(s_pg1, n + 1)
                    nc.vector.tensor_reduce(vacc[:, 1, NO2 * t:NO2 * t + NO2, :],
                                            view(prod_g, 1024 * (t % 2), [[384, NO2], [1, K1], [K1, 32]]),
                                            AX.X, ALU.add).then_inc(s_red1, 1)

            def add_channel(a, k, i):
                m = 2 * k + i
                dve.wait_ge(s_x2[m % 4], a * 128 + 16 * (m // 4 + 1))
                for j in range(NJ):
                    u = 4 * m + j
                    dve.wait_ge(s_y, a * 128 + u + 1)
                    xs = x2[:, m % 4, W * j:W * j + W]
                    nc.vector.tensor_tensor(xs, yb[u % NY][:, :], xs, ALU.add).then_inc(s_add, 1)

            def body(b, first, last):
                a = b - 1
                for s in range(STEPS):
                    pairs = pass2_pairs(b, s)
                    before, between = quad_chunks(s)
                    last_before, last_between = quad_chunks(s, LAST_CHUNKS)
                    units_before, units_between = L1_UNITS.get(s, ((), ()))
                    if first and s < 8:
                        to_staging(s)
                        if s == 7:
                            dve.wait_ge(s_w0[0], 64 * 16)
                            dve.wait_ge(s_w0[1], 64 * 16)
                    if not first:
                        if s == LAST_QUAD_STEP:
                            quad_statistics(a, NQ - 1)
                        for q, t in last_before:
                            mix_chunk(a, q, t)
                        if s == CROSS_STEP:
                            cross_terms(a, 0)
                        if s == TOTAL_STEP:
                            layer1_statistics(a)
                        layer1_mix(a, units_before)
                    if not last:
                        for q, t in before:
                            mix_chunk(b, q, t)
                        if s in QUAD_STEP:
                            quad_statistics(b, QUAD_STEP.index(s))
                    if pairs:
                        add_channel(*pairs[0], 0)
                    if not first:
                        for q, t in last_between:
                            mix_chunk(a, q, t)
                        if s == CROSS_STEP:
                            cross_terms(a, 1)
                        if s == TOTAL_STEP:
                            layer1_spectrum(a)
                        layer1_mix(a, units_between)
                    if not last:
                        for q, t in between:
                            mix_chunk(b, q, t)
                    for n, (a2, k) in enumerate(pairs):
                        if n:
                            add_channel(a2, k, 0)
                        add_channel(a2, k, 1)

            body(0, True, False)
            body(1, False, False)
            with dve.Fori(2, B) as b:
                body(b, False, False)
            body(B, False, True)

        @block.gpsimd
        def _(pool):
            def inverse_std(b, q):
                n = NQ * b + q
                pool.wait_ge(s_st, 5 * (n + 1))
                if q or not is_zero(b):
                    pool.wait_ge(s_xab, 2 * n)
                nc.gpsimd.tensor_tensor(rr0[:, 1, :], st[:, 3, :], expo[:, 0:PQ], ALU.pow).then_inc(s_rs, 1)

            def mix_chunk(b, q, t):
                n = 4 * (NQ * b + q) + t
                pool.wait_ge(s_xab, 2 * (NQ * b + q + 1))
                if q or t > 1 or not is_zero(b):
                    pool.wait_ge(s_red, 2 * (n - 1))
                pr = prod_g[:, t % 2, :].rearrange("p (o n) -> p o n", o=NO4)
                nc.gpsimd.tensor_tensor(pr, w0[:, NO4 * t:NO4 * t + NO4, q].rearrange("p o k s c -> p o (k s c)"),
                                        view(xab, 256, [[0, NO4], [1, 256]]), ALU.mult).then_inc(s_pg0, 1)

            def accumulate(b, q, t):
                n = 4 * (NQ * b + q) + t
                pool.wait_ge(s_red, 2 * (n + 1))
                if q > 1:
                    pool.wait_ge(s_tacc, 12 * b + 4 * (q - 2) + t + 1)
                c = tacc[:, :, NO4 * t:NO4 * t + NO4, :]
                nc.gpsimd.tensor_tensor(c, c, tq[:, t % 2], ALU.add).then_inc(s_tacc, 1)

            def mix_chunks(b, chunks):
                chunks = list(chunks)
                for n, (q, t) in enumerate(chunks):
                    mix_chunk(b, q, t)
                    if n and chunks[n - 1][0]:
                        accumulate(b, *chunks[n - 1])
                if chunks and chunks[-1][0]:
                    accumulate(b, *chunks[-1])

            def layer1_std(a):
                pool.wait_ge(s_st1, 5 * (a + 1))
                pool.wait_ge(s_xab1, 2 * a)
                nc.gpsimd.tensor_tensor(rr1[:, 1, :], st1[:, 0, :], expo[:, :], ALU.pow).then_inc(s_rs1, 1)

            def layer1_mix(a):
                pool.wait_ge(s_xab1, 2 * (a + 1))
                for t in range(U1):
                    n = U1 * a + t
                    if t >= 2:
                        pool.wait_ge(s_red1, 2 * (n - 1))
                    else:
                        pool.wait_ge(s_red, 32 * (a + 1))
                    pr = prod_g[:, t % 2, 0:384 * NO2].rearrange("p (o n) -> p o n", o=NO2)
                    nc.gpsimd.tensor_tensor(pr, w1[:, NO2 * t:NO2 * t + NO2].rearrange("p o s c k -> p o (s c k)"),
                                            view(xab1, 384, [[0, NO2], [1, 384]]), ALU.mult).then_inc(s_pg1, 1)

            def body(b, first, last):
                a = b - 1
                for s in range(STEPS):
                    before, between = quad_chunks(s)
                    last_before, last_between = quad_chunks(s, LAST_CHUNKS)
                    if not first:
                        if s == LAST_QUAD_STEP:
                            inverse_std(a, NQ - 1)
                        mix_chunks(a, last_before + last_between)
                        if s == TOTAL_STEP:
                            layer1_std(a)
                            if is_zero(a):
                                pool.wait_ge(s_w1, 4 * 4 * HO * 16)
                            layer1_mix(a)
                    if not last:
                        if s == QUAD_STEP[0] and not first:
                            pool.wait_ge(s_red1, 2 * U1 * b)
                        mix_chunks(b, before)
                        if s in QUAD_STEP:
                            inverse_std(b, QUAD_STEP.index(s))
                        mix_chunks(b, between)

            nc.gpsimd.memset(w1[:, :, :, :, :], 0.0).then_inc(s_zero, 1)
            nc.gpsimd.memset(prod_g[:, 0, 0:P], 0.0).then_inc(s_zero, 1)
            nc.gpsimd.memset(expo[:, :], -0.5).then_inc(s_zero, 1)
            pool.wait_ge(s_zero, 3)
            pool.wait_ge(s_w0[0], 64 * 16)
            pool.wait_ge(s_w0[1], 64 * 16)
            body(0, True, False)
            body(1, False, False)
            with pool.Fori(2, B) as b:
                body(b, False, False)
            body(B, False, True)


_INS = ["x", "L0_conv_coeff_real", "L0_conv_coeff_imag", "L0_conv_proj",
        "L1_conv_w1_real", "L1_conv_w1_imag", "L1_conv_w2_real", "L1_conv_w2_imag"]


def kernel(**inputs):
    import numpy as _np
    import concourse.bacc as _bacc
    from concourse import mybir as _mybir
    from concourse.bass_utils import run_bass_kernel_spmd as _run

    nc = _bacc.Bacc("TRN2", target_bir_lowering=False, num_devices=1, dynamic_dma_scratch_size=1024)
    arrays, args = {}, []
    for name, a in [(n, inputs[n]) for n in _INS] + [("table", constants())]:
        a = _np.ascontiguousarray(a)
        arrays[f"in_{name}_dram"] = a
        args.append(nc.dram_tensor(f"in_{name}_dram", a.shape, _mybir.dt.from_np(a.dtype), kind="ExternalInput").ap())
    args.append(nc.dram_tensor("out_0_dram", (B, C, H, W), _mybir.dt.float32, kind="ExternalOutput").ap())
    conv_preact_two_layers(nc, *args)
    r = _run(nc, [arrays], core_ids=[0])
    return r.results[0]["out_0_dram"]
```

```python
import math

import numpy as np

import concourse.bass as bass
from concourse import mybir
from contextlib import ExitStack

FP32 = mybir.dt.float32
BF16 = mybir.dt.bfloat16
ALU = mybir.AluOpType
ACT = mybir.ActivationFunctionType
AX = mybir.AxisListType

B, C, H, W = 8, 32, 512, 512
K0 = 32
K1 = 12
M1 = 2 * K1
P = 128
NJ = H // P
NW = W // P
NP = C // 2
NQ = 4
PQ = NP // NQ
HO = C // 2
GROUP = 2 * H * W
EPS = 1e-5

MATS = ["rc", "rs", "rcn", "dc", "ah", "ahr0", "ahi0", "rc1", "rs1", "rcn1", "s1", "s1r0", "s1i0",
        "qc0", "qc1", "qs0", "qs1", "qsn0", "qsn1", "pc0", "pc1", "ps0", "ps1", "psn0", "psn1", "ident"]
MAT_AT = {name: n * P for n, name in enumerate(MATS)}
SUMS = ["ones", "sums", "w8", "w4", "ysum"]
SUM_AT = {name: len(MATS) * P + n for n, name in enumerate(SUMS)}
ROW_DFT = len(MATS) * P + 8
COL_DFT = ROW_DFT + NJ * 2 * K0
ROW_INV = COL_DFT + NW * 2 * K0
COL_INV = ROW_INV + H
NCONST = COL_INV + 2 * W


def constants():
    t = np.zeros((P, NCONST), np.float64)

    def z(i, cs, k):
        return 64 * i + 32 * cs + k

    def g(o, i, k):
        return 64 * o + 32 * i + k

    def put(name, row, col, v):
        t[row, MAT_AT[name] + col] += v

    for i in range(2):
        for o in range(2):
            for k in range(K0):
                put("rc", z(i, 0, k), g(o, i, k), 1)
                put("rcn", z(i, 0, k), g(o, i, k), -1)
                put("rs", z(i, 1, k), g(o, i, k), -1)
            for i2 in range(2):
                put("dc", z(i2, 0, 0), g(o, i, 0), -0.5)
            for m in range(M1):
                j, sign = (m, -1) if m < K1 else (M1 - m, 1)
                put("rc1", z(i, 0, j), g(o, i, m), 1)
                put("rcn1", z(i, 0, j), g(o, i, m), -1)
                put("rs1", z(i, 1, j), g(o, i, m), sign)
    for o in range(2):
        for i in range(2):
            for rep in range(2):
                for k in range(K0):
                    put("ah", g(o, i, k), g(rep, o, k), 0.5)
                    put("ahr0", g(o, i, k), g(rep, o, k), 0.25 if k else 0.5)
                    put("ahi0", g(o, i, k), g(rep, o, k), 0.25 if k else 0)
                for m in range(K1):
                    put("s1", g(o, i, m), g(rep, o, m), 1)
                for m in range(1, K1):
                    put("s1r0", g(o, i, m), g(rep, o, m), 0.5)
                    put("s1i0", g(o, i, m), g(rep, o, m), 0.5)
                for m in range(K1, M1):
                    put("s1r0", g(o, i, M1 - m), g(rep, o, m), 0.5)
                    put("s1i0", g(o, i, M1 - m), g(rep, o, m), -0.5)
                for i2 in range(2):
                    put("s1r0", g(o, i, 0), g(rep, i2, 0), 0.5 if i2 == o else -0.5)
            for k in range(K0):
                put(f"qc{o}", g(o, i, k), k, 1)
                put(f"qs{o}", g(o, i, k), 64 + k, 1)
                put(f"qsn{o}", g(o, i, k), 64 + k, -1)
            for m in range(M1):
                r = m if m < K1 else K0 + m - K1
                put(f"pc{o}", g(o, i, m), r, 1)
                put(f"ps{o}", g(o, i, m), 64 + r, 1)
                put(f"psn{o}", g(o, i, m), 64 + r, -1)
    t[:, SUM_AT["ones"]] = 1
    t[:, MAT_AT["ident"]:MAT_AT["ident"] + P] = np.eye(P)
    for i in range(2):
        t[z(i, 0, 0), SUM_AT["sums"]] = 1
        t[g(0, i, 0), SUM_AT["w4"]] = -4
        t[g(0, i, 0), SUM_AT["ysum"]] = 2
    t[0:64, SUM_AT["w8"]] = 8

    def angle(a, b, n):
        return 2 * np.pi * np.mod(np.multiply.outer(a, b), n) / n

    part, kx = np.arange(P), np.arange(K0)
    for j in range(NJ):
        a = angle(NJ * part + j, kx, H)
        t[:, ROW_DFT + 64 * j:ROW_DFT + 64 * j + 64] = np.concatenate([np.cos(a), np.sin(a)], 1)
        a = angle(P * j + part, kx, W)
        t[:, COL_DFT + 64 * j:COL_DFT + 64 * j + 64] = np.concatenate([np.cos(a), np.sin(a)], 1)
        rows = np.concatenate([kx, np.arange(H - K1, H)])
        a = angle(rows, NJ * part + j, H)
        t[0:K0 + K1, ROW_INV + P * j:ROW_INV + P * j + P] = np.cos(a)
        t[64:64 + K0 + K1, ROW_INV + P * j:ROW_INV + P * j + P] = np.sin(a)
    gain = np.where(kx == 0, 1.0, 2.0)[:, None] / (H * W)
    a = angle(kx, np.arange(W), W)
    for i in range(2):
        t[64 * i:64 * i + 32, COL_INV + W * i:COL_INV + W * i + W] = gain * np.cos(a)
        t[64 * i + 32:64 * i + 64, COL_INV + W * i:COL_INV + W * i + W] = -gain * np.sin(a)
    return t.astype(np.float32)


STEPS = NP
INV_STEP = 8
LAG = INV_STEP + 1
QUAD_STEP = [9, 11, 13]
LAST_QUAD_STEP, CROSS_STEP, TOTAL_STEP = 1, 3, 4
QUAD_CHUNKS = {9: ((), (0,)), 10: ((1,), (2,)), 11: ((3,), (4,)), 12: ((5,), (6,)), 13: ((7,), (8,)),
               14: ((9,), (10,)), 15: ((11,), ())}
LAST_CHUNKS = {1: ((12,), (13,)), 2: ((14,), (15,))}
L1_UNITS = {5: ((0, 1), (2,)), 6: ((3, 4), (5,)), 7: ((6, 7), ())}
W0_STEPS = K0 // 4
W1_LATE_STEPS = 4
W1_EARLY, W1_MIDDLE, W1_LATE = 8, 14, 20
assert W0_STEPS * W1_EARLY + (STEPS - W0_STEPS) * W1_MIDDLE + W1_LATE_STEPS * W1_LATE == 4 * 4 * HO
RING2 = 3
NO4 = 4
NO2 = 2
NY = 4
U1 = HO // NO2


def conv_preact_two_layers(nc, x, coeff_re, coeff_im, proj, w1_re, w1_im, w2_re, w2_im, table, out):
    xv = x.rearrange("b c (p j) w -> b c p (j w)", j=NJ)
    ov = out.rearrange("b c (p j) w -> b c p (j w)", j=NJ)

    ctx = ExitStack()
    with ctx:
        def sb(name, shape, dt=FP32):
            return ctx.enter_context(nc.sbuf_tensor(name, shape, dt))

        def sem(name):
            return ctx.enter_context(nc.semaphore(name))

        def view(t, offset, dims, parts=P, part0=0):
            row = t[:].ap[0][0]
            return bass.AP(tensor=t[:].tensor, offset=part0 * row + offset, ap=[[row, parts], *dims])

        const = sb("const", [P, NCONST])
        w0 = sb("w0", [P, HO, NQ, K0, 2, PQ])
        w1 = sb("w1", [P, HO, 2, NP, K1])
        x1 = sb("x1", [P, 4, NJ * W])
        x2 = sb("x2", [P, RING2 + 2, NJ * W])
        rows = sb("rows", [P, W])
        cols = sb("cols", [P, NW, P])
        zq = sb("zq", [P, 2 * PQ, 2, K0])
        xt = sb("xt", [P, 2, NP, K0])
        xb = sb("xb", [P, 2, NP, K1])
        junk = sb("junk", [P, 1024], BF16)
        sq = sb("sq", [P, NP, 4])
        prod_v = sb("prod_v", [P, 1024])
        prod_g = sb("prod_g", [P, 1024])
        tacc = sb("tacc", [P, 2, HO, K0])
        tq = sb("tq", [P, 2, 2, NO4, K0])
        xab1 = sb("xab1", [P, 2, 2, NP, K1])
        xab = xab1
        vacc = tq[:, :, :, :, :].rearrange("p a b o k -> p (a b o k)")[:, 0:2 * HO * K1]\
            .rearrange("p (r o k) -> p r o k", r=2, k=K1)
        csb = sb("csb", [P, NP, 2, 2, K0])
        gsb = sb("gsb", [P, H])
        st = sb("st", [P, 5, PQ])
        var0 = sb("var0", [P, NP])
        rr0 = sb("rr0", [P, 2, PQ])
        st1 = sb("st1", [P, 4, NP])
        rr1 = sb("rr1", [P, 2, NP])
        dq = sb("dq", [P, 2, NP])
        expo = sb("expo", [P, NP])
        ah = prod_g[:, :].rearrange("p (r n) -> p r n", r=2)

        def bank(name):
            return ctx.enter_context(nc.psum_tensor(name, [P, 512], FP32))

        fa = bank("fa")
        ft = bank("ft")
        zb = bank("zb")
        mid = bank("mid")
        yb = [bank(f"y{n}") for n in range(NY)]

        def mat(name):
            return const[:, MAT_AT[name]:MAT_AT[name] + P]

        def total(name):
            return const[:, SUM_AT[name]:SUM_AT[name] + 1].broadcast_to([P, P])

        row_dft = const[:, ROW_DFT:COL_DFT].rearrange("p (j n) -> p j n", j=NJ)
        col_dft = const[:, COL_DFT:ROW_INV].rearrange("p (j n) -> p j n", j=NW)
        row_inv = const[:, ROW_INV:COL_INV]
        col_inv = const[:, COL_INV:NCONST].rearrange("p (i w) -> p i w", i=2)

        coef = [x2[:, n, :].rearrange("p (r n) -> p r n", r=2) for n in (0, 1)]
        wst = [x2[:, n, :].rearrange("p (i q k s c) -> p i q k s c", i=2, q=NQ, k=K0, s=2) for n in (2, 3)]
        projb = prod_g[:, 0:P]

        s_const = sem("s_const")
        s_zero = sem("s_zero")
        s_proj = sem("s_proj")
        s_w1 = sem("s_w1")
        s_coef = [sem("s_coef0"), sem("s_coef1")]
        s_wc = sem("s_wc")
        s_wst = sem("s_wst")
        s_w0 = [sem("s_w0a"), sem("s_w0b")]
        s_w0p = [sem("s_w0pa"), sem("s_w0pb")]
        s_x1 = [sem(f"s_x1_{n}") for n in range(4)]
        s_x2 = [sem(f"s_x2_{n}") for n in range(RING2 + 2)]
        s_out = [sem(f"s_out_{n}") for n in range(RING2 + 2)]
        s_out1 = [sem(f"s_out1_{n}") for n in range(4)]
        s_fa = sem("s_fa")
        s_sq = sem("s_sq")
        s_junk = sem("s_junk")
        s_rows = sem("s_rows")
        s_ft = sem("s_ft")
        s_cols = sem("s_cols")
        s_zb = sem("s_zb")
        s_zq = sem("s_zq")
        s_quad = sem("s_quad")
        s_keep = sem("s_keep")
        s_st = sem("s_st")
        s_rs = sem("s_rs")
        s_rr = sem("s_rr")
        s_xab = sem("s_xab")
        s_pv0 = sem("s_pv0")
        s_pg0 = sem("s_pg0")
        s_red = sem("s_red")
        s_tacc = sem("s_tacc")
        s_cross = sem("s_cross")
        s_ah = sem("s_ah")
        s_cadd = sem("s_cadd")
        s_cmul = sem("s_cmul")
        s_cred = sem("s_cred")
        s_tot = sem("s_tot")
        s_st1 = sem("s_st1")
        s_rs1 = sem("s_rs1")
        s_rr1 = sem("s_rr1")
        s_cc = sem("s_cc")
        s_ccc = sem("s_ccc")
        s_l1 = sem("s_l1")
        s_x1s = sem("s_x1s")
        s_xab1 = sem("s_xab1")
        s_pv1 = sem("s_pv1")
        s_pg1 = sem("s_pg1")
        s_red1 = sem("s_red1")
        s_gp = sem("s_gp")
        s_gs = sem("s_gs")
        s_y = sem("s_y")
        s_add = sem("s_add")

        block = ctx.enter_context(nc.Block())

        def is_zero(b):
            return isinstance(b, int) and b == 0

        def is_one(b):
            return isinstance(b, int) and b == 1

        def pass2_pairs(b, s):
            if is_zero(b) or is_one(b) and s < LAG:
                return []
            if s < LAG:
                return [(b - 2, NP - LAG + s)]
            if isinstance(b, int) and b == B:
                return [(b - 1, k) for k in range(NP)] if s == LAG else []
            return [(b - 1, s - LAG)]

        def pair_of(a, k):
            if isinstance(a, int) and a == B - 1:
                return NP - 1 - k if k < 2 else k - 2
            return (k + NP - 1) % NP

        def slot1(b, s, i):
            if s == NP - 1:
                return x2[:, RING2 + i, :], s_x2[RING2 + i], b * 16 + 16
            n = 2 * (s % 2) + i
            return x1[:, n, :], s_x1[n], b * (16 * (NP // 2 - s % 2)) + 16 * (s // 2 + 1)

        def slot2(a, m):
            last = isinstance(a, int) and a == B - 1
            if m < 2:
                n, count = RING2 + m, a * 16 + 16
                return x2[:, n, :], s_x2[n], count, s_out[n], count
            if last and m < 4:
                return x1[:, m - 2, :], s_x1[m - 2], B * 128, s_out1[m - 2], 16
            if not last and not (isinstance(a, int) and a == B - 2 and m >= 2 * (NP - LAG)):
                n, count = (m - 2) % RING2, a * (16 * (C - 2) // RING2) + 16 * ((m - 2) // RING2 + 1)
                return x2[:, n, :], s_x2[n], count, s_out[n], count
            t = 2 * LAG + m - 4 if last else m - 2 * (NP - LAG)
            n, use = t % (RING2 + 2), t // (RING2 + 2) + 1
            if n < RING2:
                count = (B - 2) * (16 * (C - 2) // RING2) + 16 * ((2 * (NP - LAG) - 2) // RING2 + use)
                return x2[:, n, :], s_x2[n], count, s_out[n], count
            n += 2 - RING2
            return x1[:, n, :], s_x1[n], B * 112 + 16 * use, s_out1[n], 16 * use

        def quad_chunks(s, table=QUAD_CHUNKS):
            return [[(n // 4, n % 4) for n in part] for part in table.get(s, ((), ()))]

        def w0_scatter(k, groups):
            for kg in groups:
                for o in range(2):
                    for i in range(2):
                        part = 64 * o + 32 * i + 8 * kg + k
                        src = wst[k % 2][32 * kg + o:32 * kg + 32:2, i].rearrange("p q k s c -> p (q k s c)")
                        dst = w0[part:part + 1].rearrange("p o q k s c -> p o (q k s c)")
                        yield dst, src

        def w1_loads(first, count):
            for d in range(first, first + count):
                n, o, i, ho = d // 64, d // 32 % 2, d // 16 % 2, d % 16
                src = (w1_re, w1_im, w2_re, w2_im)[n]
                part = 64 * o + 32 * i + K1 * (n // 2)
                yield w1[part:part + K1, ho, n % 2], src[i::2, 2 * ho + o].rearrange("c x y -> x c y")

        @block.sync
        def _(sp):
            def load_pass1(b, s):
                if s == NP - 1:
                    if is_zero(b):
                        for scattered in (*s_w0, *s_w0p):
                            sp.wait_ge(scattered, W0_STEPS // 2 * 8 * 16)
                elif s != 1 and not (s == 0 and is_zero(b)):
                    sp.wait_ge(s_fa, b * NP + s - 1)
                    sp.wait_ge(s_sq, b * NP + s - 1)
                for i in range(2):
                    dst, loaded, count = slot1(b, s, i)
                    if s == NP - 1 and not is_zero(b):
                        sp.wait_ge(s_out[RING2 + i], b * 16)
                    sp.dma_start(dst, xv[b, 2 * s + i]).then_inc(loaded, 16)

            def load_pass2(a, k, channels=(0, 1)):
                last = isinstance(a, int) and a == B - 1
                if k == 0 or last and k == 1:
                    return
                for i in channels:
                    dst, loaded, _, stored, count = slot2(a, 2 * k + i)
                    if isinstance(count, int) and count == 16 and not is_zero(a):
                        sp.wait_ge(s_fa, B * NP - 2)
                        sp.wait_ge(s_sq, B * NP - 2)
                    elif 2 * k + i >= 2 + RING2 or not is_zero(a):
                        sp.wait_ge(stored, count - 16)
                    sp.dma_start(dst, xv[a, 2 * pair_of(a, k) + i]).then_inc(loaded, 16)

            def load_w1(first, count):
                for dst, src in w1_loads(first, count):
                    sp.dma_start(dst, src, allow_slow_non_contiguous=True).then_inc(s_w1, 16)

            sp.dma_start(const[:, :], table).then_inc(s_const, 16)

            def load_coef(k):
                n = k % 2
                if k >= 2:
                    sp.wait_ge(s_wc, 4 * (k - 1))
                for r, src in enumerate((coeff_re, coeff_im)):
                    sp.dma_start(coef[n][:, r, :],
                                 src.rearrange("r (g k) j c -> k (r g) (j c)", k=W0_STEPS)[k]).then_inc(s_coef[n], 16)

            def scatter_w0(k):
                sp.wait_ge(s_wst, 8 * (k + 1))
                for dst, src in w0_scatter(k, (0, 1)):
                    sp.dma_start(dst, src).then_inc(s_w0[k % 2], 16)

            def body(b):
                last = isinstance(b, int) and b == B - 1
                for s in range(STEPS):
                    for a, k in pass2_pairs(b, s):
                        load_pass2(a, k, [0])
                    if s + 1 < STEPS:
                        load_pass1(b, s + 1)
                    elif not last:
                        load_pass1(b + 1, 0)
                    if is_one(b) and s < W1_LATE_STEPS:
                        load_w1(W0_STEPS * W1_EARLY + (STEPS - W0_STEPS) * W1_MIDDLE + W1_LATE * s, W1_LATE)
                    for a, k in pass2_pairs(b, s):
                        load_pass2(a, k, [1])

            load_coef(0)
            load_pass1(0, 0)
            load_coef(1)
            for s in range(STEPS):
                if s + 1 < STEPS:
                    load_pass1(0, s + 1)
                else:
                    load_pass1(1, 0)
                if 1 <= s <= W0_STEPS:
                    scatter_w0(s - 1)
                    if s + 1 < W0_STEPS:
                        load_coef(s + 1)
                if s == 0:
                    sp.wait_ge(s_zero, 3)
                if s < W0_STEPS:
                    load_w1(W1_EARLY * s, W1_EARLY)
                else:
                    load_w1(W0_STEPS * W1_EARLY + W1_MIDDLE * (s - W0_STEPS), W1_MIDDLE)
            body(1)
            with sp.Fori(2, B - 1) as b:
                body(b)
            body(B - 1)
            for s in range(STEPS):
                for a, k in pass2_pairs(B, s):
                    load_pass2(a, k)

        @block.tensor
        def _(pe):
            def wc_products(k):
                pe.wait_ge(s_coef[k % 2], 2 * 16 * (k // 2 + 1))
                for r in range(2):
                    for hh in range(2):
                        u = 4 * k + 2 * r + hh
                        if u >= NY:
                            pe.wait_ge(s_wst, 2 * (u - NY + 1))
                        nc.tensor.matmul(yb[u % NY][:, :], projb, coef[k % 2][:, r, 512 * hh:512 * hh + 512],
                                         start=True, stop=True).then_inc(s_wc, 1)

            def transposes(b, s):
                pe.wait_ge(s_rows, b * NP + s + 1)
                if s > 0 or not is_zero(b):
                    pe.wait_ge(s_cols, b * NP + s)
                for w in range(NW):
                    last = nc.tensor.transpose(ft[:, P * w:P * w + P], rows[:, P * w:P * w + P], mat("ident"))
                last.then_inc(s_ft, 1)

            def row_transform(b, s):
                if s or not is_zero(b):
                    pe.wait_ge(s_rows, b * NP + s)
                xs = [slot1(b, s, i) for i in range(2)]
                for _, loaded, count in xs:
                    pe.wait_ge(loaded, count)
                for j in range(NJ):
                    for i in range(2):
                        last = nc.tensor.matmul(fa[64 * i:64 * i + 64, :], row_dft[:, j, :],
                                                xs[i][0][:, W * j:W * j + W],
                                                start=(j == 0), stop=(j == NJ - 1))
                last.then_inc(s_fa, 1)

            def col_transform(b, s):
                pe.wait_ge(s_cols, b * NP + s + 1)
                if s or not is_zero(b):
                    pe.wait_ge(s_zq, b * NP + s)
                for w in range(NW):
                    last = nc.tensor.matmul(zb[:, 0:2 * K0], cols[:, w, :], col_dft[:, w, :],
                                            start=(w == 0), stop=(w == NW - 1))
                last.then_inc(s_zb, 1)

            def quad_spectra(b, q):
                pe.wait_ge(s_zq, b * NP + PQ * (q + 1))
                pe.wait_ge(s_sq, b * NP + PQ * (q + 1))
                if q == 0 and not is_zero(b):
                    pe.wait_ge(s_ccc, 4 * b)
                if q:
                    pe.wait_ge(s_keep, 2 * (NQ * b + q))
                    pe.wait_ge(s_xab, 2 * (NQ * b + q))
                z = zq[:, PQ * (q % 2):PQ * (q % 2) + PQ]
                nc.tensor.matmul(mid[:, 0:16], total("ones"), sq[:, PQ * q:PQ * q + PQ, :], start=True, stop=True)
                nc.tensor.matmul(mid[:, 16:20], total("sums"), z[:, :, 0, 0], start=True, stop=True)
                for at, n, c, sn, cn in ((128, K0, "rc", "rs", "rcn"), (384, K1, "rc1", "rs1", "rcn1")):
                    re = mid[:, at:at + PQ * n]
                    im = mid[:, at + PQ * n:at + 2 * PQ * n]
                    nc.tensor.matmul(re, mat(c), z[:, :, 0, 0:n], start=True, stop=False)
                    nc.tensor.matmul(re, mat(sn), z[:, :, 1, 0:n], start=False, stop=False)
                    nc.tensor.matmul(re.rearrange("p (a k) -> p a k", k=n)[:, :, 0], mat("dc"), z[:, :, 0, 0],
                                     start=False, stop=True)
                    nc.tensor.matmul(im, mat(sn), z[:, :, 0, 0:n], start=True, stop=False)
                    last = nc.tensor.matmul(im, mat(cn), z[:, :, 1, 0:n], start=False, stop=True)
                last.then_inc(s_quad, 1)

            def cross_spectra(a, r):
                if r:
                    pe.wait_ge(s_ah, 2 * a + 1)
                    pe.wait_ge(s_cadd, 2 * a + 1)
                else:
                    pe.wait_ge(s_keep, 2 * NQ * (a + 1))
                    pe.wait_ge(s_xab, 2 * NQ * (a + 1))
                    pe.wait_ge(s_red, 32 * (a + 1))
                    pe.wait_ge(s_tacc, 12 * (a + 1))
                m3 = mid[:, :].rearrange("p (a k) -> p a k", k=K0)
                nc.tensor.matmul(m3[:, :, 1:K0], mat("ah"), tacc[:, r, :, 1:K0], start=True, stop=True)
                nc.tensor.matmul(m3[:, :, 0], mat("ahi0" if r else "ahr0"), tacc[:, r, :, 0], start=True, stop=True)\
                    .then_inc(s_cross, 1)

            def cross_totals(a):
                pe.wait_ge(s_cred, 2 * (a + 1))
                pe.wait_ge(s_ah, 2 * (a + 1))
                nc.tensor.matmul(mid[:, 0:NP], total("w8"), dq[:, 0, :], start=True, stop=False)
                nc.tensor.matmul(mid[:, 0:NP], total("w8"), dq[:, 1, :], start=False, stop=False)
                p0 = prod_v[:, 0:512].rearrange("p (a k) -> p a k", k=K0)
                nc.tensor.matmul(mid[:, 0:NP], total("w4"), p0[:, :, 0], start=False, stop=True)
                a0 = ah[:, 0, :].rearrange("p (a k) -> p a k", k=K0)
                nc.tensor.matmul(mid[:, NP:2 * NP], total("ysum"), a0[:, :, 0], start=True, stop=True)\
                    .then_inc(s_tot, 1)

            def layer1_input(a):
                pe.wait_ge(s_st1, 5 * a + 2)
                for r, col0 in enumerate(("s1r0", "s1i0")):
                    m3 = mid[:, 192 * r:192 * r + 192].rearrange("p (a k) -> p a k", k=K1)
                    nc.tensor.matmul(m3[:, :, 1:K1], mat("s1"), tacc[:, r, :, 1:K1], start=True, stop=True)
                    last = nc.tensor.matmul(m3[:, :, 0], mat(col0), tacc[:, r, :, 0], start=True, stop=True)
                last.then_inc(s_l1, 1)

            def inverse_input(a, u):
                o, r = u // 2, u % 2
                if u:
                    pe.wait_ge(s_ccc, 4 * a + u)
                else:
                    pe.wait_ge(s_x1s, a + 1)
                    pe.wait_ge(s_red1, 2 * U1 * (a + 1))
                m3 = mid[:, :].rearrange("p (a k) -> p a k", k=K0)[:, :, 0:K1]
                q_turn, p_turn = ("qs", "ps") if r else ("qsn", "psn")
                nc.tensor.matmul(mid[:, :], mat(f"qc{o}"), tacc[:, r], start=True, stop=False)
                nc.tensor.matmul(mid[:, :], mat(f"{q_turn}{o}"), tacc[:, 1 - r], start=False, stop=False)
                nc.tensor.matmul(m3, mat(f"pc{o}"), vacc[:, r], start=False, stop=False)
                nc.tensor.matmul(m3, mat(f"{p_turn}{o}"), vacc[:, 1 - r], start=False, stop=True).then_inc(s_cc, 1)

            def inverse_rows(a, k, transposed):
                if k == 0:
                    pe.wait_ge(s_ccc, 4 * (a + 1))
                if k or not is_zero(a):
                    pe.wait_ge(s_gs, a * NP + k)
                pe.wait_ge(s_cols, transposed)
                nc.tensor.matmul(ft[:, :], csb[:, pair_of(a, k)].rearrange("p i r k -> p (i r k)"), row_inv,
                                 start=True, stop=True).then_inc(s_gp, 1)

            def inverse_cols(a, k, i):
                if i == 0:
                    pe.wait_ge(s_gs, a * NP + k + 1)
                for j in range(NJ):
                    u = 8 * k + 4 * i + j
                    if u >= NY or not is_zero(a):
                        pe.wait_ge(s_add, a * 128 + max(u - NY + 1, 0))
                    nc.tensor.matmul(yb[u % NY][:, :], gsb[:, P * j:P * j + P],
                                     col_inv[:, i, :], start=True, stop=True).then_inc(s_y, 1)

            def body(b, first, last):
                a = b - 1
                for s in range(STEPS):
                    earlier = (s or not first) and not (last and s)
                    pairs = pass2_pairs(b, s)
                    if pairs:
                        inverse_rows(*pairs[0], b * NP if last and s else b * NP + s - 1)
                    if not last:
                        row_transform(b, s)
                    if not first:
                        if s == LAST_QUAD_STEP:
                            quad_spectra(a, NQ - 1)
                        if s == CROSS_STEP:
                            cross_spectra(a, 0)
                        if s == TOTAL_STEP:
                            cross_totals(a)
                        if s == INV_STEP:
                            inverse_input(a, 0)
                    if not last and s in QUAD_STEP:
                        quad_spectra(b, QUAD_STEP.index(s))
                    if pairs:
                        inverse_cols(*pairs[0], 0)
                    if earlier:
                        transposes(b, s - 1)
                    if not first:
                        if s == CROSS_STEP:
                            cross_spectra(a, 1)
                        if s == TOTAL_STEP:
                            layer1_input(a)
                        if s == INV_STEP:
                            inverse_input(a, 1)
                    for n, (a2, k) in enumerate(pairs):
                        if n:
                            inverse_cols(a2, k, 0)
                        if n + 1 < len(pairs):
                            inverse_rows(*pairs[n + 1], b * NP)
                        inverse_cols(a2, k, 1)
                    if not first and s == INV_STEP:
                        inverse_input(a, 2)
                    if earlier:
                        col_transform(b, s - 1)
                    if first and s < W0_STEPS:
                        if s == 0:
                            pe.wait_ge(s_proj, 4 * 16)
                        wc_products(s)
                    if not first and s == INV_STEP:
                        inverse_input(a, 3)
            pe.wait_ge(s_const, 16)
            body(0, True, False)
            body(1, False, False)
            with pe.Fori(2, B) as b:
                body(b, False, False)
            body(B, False, True)

        @block.scalar
        def _(act):
            def copy(dst, src):
                return nc.scalar.activation(dst, src, ACT.Copy)

            def squares(b, s):
                for i in range(2):
                    xs, loaded, count = slot1(b, s, i)
                    act.wait_ge(loaded, count)
                    if i == 0 and not is_zero(b):
                        act.wait_ge(s_quad, NQ * (b - 1) + s // PQ + 1)
                    for hh in range(2):
                        if i or hh:
                            act.wait_ge(s_junk, 3 * NP * b + 3 * s + 2 * i + hh)
                        elif s or not is_zero(b):
                            act.wait_ge(s_sq, NP * b + s)
                        last = nc.scalar.activation(junk[:, :], xs[:, 1024 * hh:1024 * hh + 1024], ACT.Square,
                                                    accum_out=sq[:, s, 2 * i + hh:2 * i + hh + 1])
                        if i == 0 or hh == 0:
                            last.then_inc(s_junk, 1)
                last.then_inc(s_sq, 1)

            def copy_rows(b, s):
                act.wait_ge(s_fa, b * NP + s + 1)
                if s or not is_zero(b):
                    act.wait_ge(s_ft, b * NP + s)
                copy(rows[:, :], fa[:, :]).then_inc(s_rows, 1)

            def copy_cols(b, s):
                act.wait_ge(s_ft, b * NP + s + 1)
                if s or not is_zero(b):
                    act.wait_ge(s_zb, b * NP + s)
                copy(cols[:, :, :].rearrange("p a b -> p (a b)"), ft[:, :]).then_inc(s_cols, 1)

            def copy_spectrum(b, s):
                act.wait_ge(s_zb, b * NP + s + 1)
                if s >= 8 or not is_zero(b):
                    act.wait_ge(s_quad, NQ * b + (s - 8) // PQ + 1)
                copy(zq[:, s % (2 * PQ)].rearrange("p t k -> p (t k)"), zb[:, 0:2 * K0]).then_inc(s_zq, 1)

            def keep_quad(b, q):
                act.wait_ge(s_quad, NQ * b + q + 1)
                if q == 0 and not is_zero(b):
                    act.wait_ge(s_xab1, 2 * b)
                for dst, at, n in ((xt, 128, K0), (xb, 384, K1)):
                    copy(dst[:, :, PQ * q:PQ * q + PQ, :],
                         mid[:, at:at + 2 * PQ * n].rearrange("p (r a k) -> p r a k", r=2, k=n)).then_inc(s_keep, 1)

            def copy_cross(a, r):
                act.wait_ge(s_cross, 2 * a + r + 1)
                copy(ah[:, r, :], mid[:, :]).then_inc(s_ah, 1)

            def copy_inverse_input(a, u):
                o, r = u // 2, u % 2
                if u == 0:
                    act.wait_ge(s_gp, NP * a)
                act.wait_ge(s_cc, 4 * a + u + 1)
                copy(csb[:, :, o, r, :], mid[:, :].rearrange("p (a k) -> p a k", k=K0)).then_inc(s_ccc, 1)

            def copy_inverse_rows(a, k):
                act.wait_ge(s_gp, a * NP + k + 1)
                act.wait_ge(s_y, a * 128 + 8 * k)
                copy(gsb[:, :], ft[:, :]).then_inc(s_gs, 1)

            def store(a, k, i):
                m = 2 * k + i
                act.wait_ge(s_add, a * 128 + 4 * (m + 1))
                src, _, _, stored, _ = slot2(a, m)
                act.dma_start(ov[a, 2 * pair_of(a, k) + i], src).then_inc(stored, 16)

            def body(b, first, last):
                a = b - 1
                for s in range(STEPS):
                    earlier = (s or not first) and not (last and s)
                    pairs = pass2_pairs(b, s)
                    if pairs:
                        copy_inverse_rows(*pairs[0])
                    if not last:
                        squares(b, s)
                    if not first:
                        if s == LAST_QUAD_STEP:
                            keep_quad(a, NQ - 1)
                        if s == CROSS_STEP:
                            copy_cross(a, 0)
                        if s == INV_STEP:
                            copy_inverse_input(a, 0)
                    if not last and s in QUAD_STEP:
                        keep_quad(b, QUAD_STEP.index(s))
                    if earlier:
                        copy_cols(b, s - 1)
                    if not last:
                        copy_rows(b, s)
                    if not first:
                        if s == CROSS_STEP:
                            copy_cross(a, 1)
                        if s == INV_STEP:
                            copy_inverse_input(a, 1)
                            copy_inverse_input(a, 2)
                    if earlier:
                        copy_spectrum(b, s - 1)
                    if not first and s == INV_STEP:
                        copy_inverse_input(a, 3)
                    for n, (a2, k) in enumerate(pairs):
                        if n + 1 < len(pairs):
                            store(a2, k, 0)
                            copy_inverse_rows(*pairs[n + 1])
                            store(a2, k, 1)
                        else:
                            store(a2, k, 0)
                            store(a2, k, 1)

            act.wait_ge(s_zero, 2)
            for kg in range(4):
                act.dma_start(prod_g[kg:P:4, 32 * kg:32 * kg + 32],
                              proj.rearrange("o r -> r o"), allow_slow_non_contiguous=True).then_inc(s_proj, 16)
            body(0, True, False)
            body(1, False, False)
            with act.Fori(2, B) as b:
                body(b, False, False)
            body(B, False, True)
            for m in (0, 1, 2, 3, *range(C - RING2 - 2, C)):
                _, _, _, stored, count = slot2(B - 1, m)
                act.wait_ge(stored, count)

        @block.vector
        def _(dve):
            def to_staging(k):
                if k >= 2:
                    dve.wait_ge(s_w0[k % 2], 8 * 16 * (k // 2))
                    dve.wait_ge(s_w0p[k % 2], 8 * 16 * (k // 2))
                for r in range(2):
                    for hh in range(2):
                        u = 4 * k + 2 * r + hh
                        dve.wait_ge(s_wc, u + 1)
                        for i in range(2):
                            src = yb[u % NY][:, :].rearrange("p (k q c i) -> p i q k c", q=NQ, c=PQ, i=2)[:, i]
                            dst = wst[k % 2][:, i, :, 16 * hh:16 * hh + 16, r, :]
                            nc.vector.tensor_copy(dst, src).then_inc(s_wst, 1)

            def quad_statistics(b, q):
                n = NQ * b + q
                dve.wait_ge(s_keep, 2 * (n + 1))
                nc.vector.tensor_reduce(st[:, 0, :], mid[:, 0:16].rearrange("p (a n) -> p a n", n=4), AX.X, ALU.add)\
                    .then_inc(s_st, 1)
                nc.vector.tensor_scalar(st[:, 1, :], mid[:, 16:20], 1.0 / GROUP, None, ALU.mult).then_inc(s_st, 1)
                dve.wait_ge(s_st, 5 * n + 2)
                nc.vector.tensor_tensor(st[:, 2, :], st[:, 1, :], st[:, 1, :], ALU.mult).then_inc(s_st, 1)
                dve.wait_ge(s_st, 5 * n + 3)
                v = var0[:, PQ * q:PQ * q + PQ]
                nc.vector.scalar_tensor_tensor(v, st[:, 0, :], 1.0 / GROUP, st[:, 2, :], ALU.mult, ALU.subtract)\
                    .then_inc(s_st, 1)
                dve.wait_ge(s_st, 5 * n + 4)
                nc.vector.tensor_scalar(st[:, 3, :], v, 0.0, EPS, ALU.max, ALU.add).then_inc(s_st, 1)
                dve.wait_ge(s_rs, n + 1)
                nc.vector.tensor_scalar(rr0[:, 0, :], rr0[:, 1, :], -1.0, None, ALU.mult).then_inc(s_rr, 1)
                if q == 0 and not is_zero(b):
                    dve.wait_ge(s_pg1, U1 * b)
                    dve.wait_ge(s_pv1, U1 * b)
                if q or not is_zero(b):
                    dve.wait_ge(s_pg0, 4 * n)
                    dve.wait_ge(s_pv0, 4 * n)
                dve.wait_ge(s_rr, n + 1)
                nc.vector.tensor_tensor(view(xab, 0, [[260, 2], [1, PQ], [8, K0]]),
                                        view(mid, 128, [[0, 2], [K0, PQ], [1, K0]]),
                                        view(rr0, PQ, [[0, 2], [1, PQ], [0, K0]]), ALU.mult).then_inc(s_xab, 1)
                nc.vector.tensor_tensor(view(xab, 4, [[252, 2], [1, PQ], [8, K0]]),
                                        view(mid, 256, [[0, 2], [K0, PQ], [1, K0]]),
                                        view(rr0, 0, [[PQ, 2], [1, PQ], [0, K0]]), ALU.mult).then_inc(s_xab, 1)

            def mix_chunk(b, q, t):
                n = 4 * (NQ * b + q) + t
                if q:
                    dst = tq[:, t % 2]
                    if q > 1 or t > 1:
                        dve.wait_ge(s_tacc, 12 * b + 4 * (q - 1) + t - 1)
                    elif not is_zero(b):
                        dve.wait_ge(s_tacc, 12 * b)
                else:
                    dst = tacc[:, :, NO4 * t:NO4 * t + NO4, :]
                    if not is_zero(b) and t == 0:
                        dve.wait_ge(s_cc, 4 * b)
                dve.wait_ge(s_xab, 2 * (NQ * b + q + 1))
                if q or t:
                    dve.wait_ge(s_red, 2 * n - 1)
                elif not is_zero(b):
                    dve.wait_ge(s_red1, 2 * U1 * b)
                pr = prod_v[:, :].rearrange("p (o n) -> p o n", o=NO4)
                nc.vector.tensor_tensor(pr, w0[:, NO4 * t:NO4 * t + NO4, q].rearrange("p o k s c -> p o (k s c)"),
                                        view(xab, 0, [[0, NO4], [1, 256]]), ALU.mult).then_inc(s_pv0, 1)
                dve.wait_ge(s_pv0, n + 1)
                nc.vector.tensor_reduce(dst[:, 0], prod_v[:, :].rearrange("p (o k n) -> p o k n", o=NO4, k=K0),
                                        AX.X, ALU.add).then_inc(s_red, 1)
                dve.wait_ge(s_pg0, n + 1)
                nc.vector.tensor_reduce(dst[:, 1],
                                        prod_g[:, :].rearrange("p (o k n) -> p o k n", o=NO4, k=K0),
                                        AX.X, ALU.add).then_inc(s_red, 1)

            def cross_terms(a, r):
                if r == 0:
                    dve.wait_ge(s_keep, 2 * NQ * (a + 1))
                    dve.wait_ge(s_red, 8 * NQ * (a + 1))
                c = prod_v[:, 512 * r:512 * r + 512]
                dve.wait_ge(s_ah, 2 * a + r + 1)
                nc.vector.tensor_tensor(c, mid[:, :], xt[:, r].rearrange("p a k -> p (a k)"), ALU.add)\
                    .then_inc(s_cadd, 1)
                dve.wait_ge(s_cadd, 2 * a + r + 1)
                nc.vector.tensor_tensor(c, c, ah[:, r, :], ALU.mult).then_inc(s_cmul, 1)
                dve.wait_ge(s_cmul, 2 * a + r + 1)
                nc.vector.tensor_reduce(dq[:, r, :], c.rearrange("p (a k) -> p a k", k=K0), AX.X, ALU.add)\
                    .then_inc(s_cred, 1)

            def layer1_statistics(a):
                dve.wait_ge(s_tot, a + 1)
                nc.vector.scalar_tensor_tensor(st1[:, 0, :], mid[:, 0:NP], 1.0 / (GROUP * H * W), var0[:, :],
                                               ALU.mult, ALU.add).then_inc(s_st1, 1)
                nc.vector.tensor_scalar(st1[:, 1, :], mid[:, NP:2 * NP], 1.0 / GROUP, None, ALU.mult)\
                    .then_inc(s_st1, 1)
                dve.wait_ge(s_st1, 5 * a + 2)
                nc.vector.tensor_tensor(st1[:, 2, :], st1[:, 1, :], st1[:, 1, :], ALU.mult).then_inc(s_st1, 1)
                dve.wait_ge(s_st1, 5 * a + 3)
                nc.vector.tensor_tensor(st1[:, 3, :], st1[:, 0, :], st1[:, 2, :], ALU.subtract).then_inc(s_st1, 1)
                dve.wait_ge(s_st1, 5 * a + 4)
                nc.vector.tensor_scalar(st1[:, 0, :], st1[:, 3, :], 0.0, EPS, ALU.max, ALU.add).then_inc(s_st1, 1)
                dve.wait_ge(s_rs1, a + 1)
                nc.vector.tensor_scalar(rr1[:, 0, :], rr1[:, 1, :], -1.0, None, ALU.mult).then_inc(s_rr1, 1)

            def layer1_spectrum(a):
                dve.wait_ge(s_l1, a + 1)
                flat = xb[:, :, :, :].rearrange("p r a k -> p (r a k)")
                nc.vector.tensor_tensor(flat, flat, mid[:, 0:384], ALU.add).then_inc(s_x1s, 1)
                dve.wait_ge(s_x1s, a + 1)
                dve.wait_ge(s_rr1, a + 1)
                dve.wait_ge(s_pg0, 4 * NQ * (a + 1))
                dve.wait_ge(s_pv0, 4 * NQ * (a + 1))
                nc.vector.tensor_tensor(view(xab1, 0, [[576, 2], [K1, NP], [1, K1]]),
                                        view(xb, 0, [[0, 2], [K1, NP], [1, K1]]),
                                        view(rr1, NP, [[0, 2], [1, NP], [0, K1]]), ALU.mult).then_inc(s_xab1, 1)
                nc.vector.tensor_tensor(view(xab1, 192, [[192, 2], [K1, NP], [1, K1]]),
                                        view(xb, 192, [[0, 2], [K1, NP], [1, K1]]),
                                        view(rr1, 0, [[NP, 2], [1, NP], [0, K1]]), ALU.mult).then_inc(s_xab1, 1)

            def layer1_mix(a, units):
                for t in units:
                    n = U1 * a + t
                    if t:
                        dve.wait_ge(s_red1, 2 * n - 1)
                    else:
                        dve.wait_ge(s_cred, 2 * (a + 1))
                        dve.wait_ge(s_xab1, 2 * (a + 1))
                        if is_zero(a):
                            dve.wait_ge(s_w1, 4 * 4 * HO * 16)
                    pr = prod_v[:, 0:384 * NO2].rearrange("p (o n) -> p o n", o=NO2)
                    nc.vector.tensor_tensor(pr, w1[:, NO2 * t:NO2 * t + NO2].rearrange("p o s c k -> p o (s c k)"),
                                            view(xab1, 0, [[0, NO2], [1, 384]]), ALU.mult).then_inc(s_pv1, 1)
                    dve.wait_ge(s_pv1, n + 1)
                    nc.vector.tensor_reduce(vacc[:, 0, NO2 * t:NO2 * t + NO2, :],
                                            view(prod_v, 0, [[384, NO2], [1, K1], [K1, 32]]), AX.X, ALU.add)\
                        .then_inc(s_red1, 1)
                    dve.wait_ge(s_pg1, n + 1)
                    nc.vector.tensor_reduce(vacc[:, 1, NO2 * t:NO2 * t + NO2, :],
                                            view(prod_g, 0, [[384, NO2], [1, K1], [K1, 32]]),
                                            AX.X, ALU.add).then_inc(s_red1, 1)

            def add_channel(a, k, i):
                m = 2 * k + i
                buf, loaded, count, _, _ = slot2(a, m)
                dve.wait_ge(loaded, count)
                for j in range(NJ):
                    u = 4 * m + j
                    dve.wait_ge(s_y, a * 128 + u + 1)
                    xs = buf[:, W * j:W * j + W]
                    nc.vector.tensor_tensor(xs, yb[u % NY][:, :], xs, ALU.add).then_inc(s_add, 1)

            def body(b, first, last):
                a = b - 1
                for s in range(STEPS):
                    pairs = pass2_pairs(b, s)
                    before, between = quad_chunks(s)
                    last_before, last_between = quad_chunks(s, LAST_CHUNKS)
                    units_before, units_between = L1_UNITS.get(s, ((), ()))
                    if first and s < W0_STEPS:
                        to_staging(s)
                    if first and s == QUAD_STEP[0]:
                        for scattered in (*s_w0, *s_w0p):
                            dve.wait_ge(scattered, W0_STEPS // 2 * 8 * 16)
                    if not first:
                        if s == LAST_QUAD_STEP:
                            quad_statistics(a, NQ - 1)
                        for q, t in last_before:
                            mix_chunk(a, q, t)
                        if s == CROSS_STEP:
                            cross_terms(a, 0)
                        if s == TOTAL_STEP:
                            layer1_statistics(a)
                        layer1_mix(a, units_before)
                    if not last:
                        for q, t in before:
                            mix_chunk(b, q, t)
                        if s in QUAD_STEP:
                            quad_statistics(b, QUAD_STEP.index(s))
                    if pairs:
                        add_channel(*pairs[0], 0)
                    if not first:
                        for q, t in last_between:
                            mix_chunk(a, q, t)
                        if s == CROSS_STEP:
                            cross_terms(a, 1)
                        if s == TOTAL_STEP:
                            layer1_spectrum(a)
                        layer1_mix(a, units_between)
                    if not last:
                        for q, t in between:
                            mix_chunk(b, q, t)
                    for n, (a2, k) in enumerate(pairs):
                        if n:
                            add_channel(a2, k, 0)
                        add_channel(a2, k, 1)

            body(0, True, False)
            body(1, False, False)
            with dve.Fori(2, B) as b:
                body(b, False, False)
            body(B, False, True)

        @block.gpsimd
        def _(pool):
            def inverse_std(b, q):
                n = NQ * b + q
                pool.wait_ge(s_st, 5 * (n + 1))
                if q or not is_zero(b):
                    pool.wait_ge(s_xab, 2 * n)
                nc.gpsimd.tensor_tensor(rr0[:, 1, :], st[:, 3, :], expo[:, 0:PQ], ALU.pow).then_inc(s_rs, 1)

            def mix_chunk(b, q, t):
                n = 4 * (NQ * b + q) + t
                pool.wait_ge(s_xab, 2 * (NQ * b + q + 1))
                if q or t or not is_zero(b):
                    pool.wait_ge(s_red, 2 * n)
                pr = prod_g[:, :].rearrange("p (o n) -> p o n", o=NO4)
                nc.gpsimd.tensor_tensor(pr, w0[:, NO4 * t:NO4 * t + NO4, q].rearrange("p o k s c -> p o (k s c)"),
                                        view(xab, 256, [[0, NO4], [1, 256]]), ALU.mult).then_inc(s_pg0, 1)

            def accumulate(b, q, t):
                n = 4 * (NQ * b + q) + t
                pool.wait_ge(s_red, 2 * (n + 1))
                if q > 1:
                    pool.wait_ge(s_tacc, 12 * b + 4 * (q - 2) + t + 1)
                c = tacc[:, :, NO4 * t:NO4 * t + NO4, :]
                nc.gpsimd.tensor_tensor(c, c, tq[:, t % 2], ALU.add).then_inc(s_tacc, 1)

            def mix_chunks(b, chunks):
                chunks = list(chunks)
                for n, (q, t) in enumerate(chunks):
                    mix_chunk(b, q, t)
                    if n and chunks[n - 1][0]:
                        accumulate(b, *chunks[n - 1])
                if chunks and chunks[-1][0]:
                    accumulate(b, *chunks[-1])

            def layer1_std(a):
                pool.wait_ge(s_st1, 5 * (a + 1))
                pool.wait_ge(s_xab1, 2 * a)
                nc.gpsimd.tensor_tensor(rr1[:, 1, :], st1[:, 0, :], expo[:, :], ALU.pow).then_inc(s_rs1, 1)

            def layer1_mix(a):
                pool.wait_ge(s_xab1, 2 * (a + 1))
                for t in range(U1):
                    n = U1 * a + t
                    if t:
                        pool.wait_ge(s_red1, 2 * n)
                    else:
                        pool.wait_ge(s_red, 32 * (a + 1))
                    pr = prod_g[:, 0:384 * NO2].rearrange("p (o n) -> p o n", o=NO2)
                    nc.gpsimd.tensor_tensor(pr, w1[:, NO2 * t:NO2 * t + NO2].rearrange("p o s c k -> p o (s c k)"),
                                            view(xab1, 384, [[0, NO2], [1, 384]]), ALU.mult).then_inc(s_pg1, 1)

            def body(b, first, last):
                a = b - 1
                for s in range(STEPS):
                    before, between = quad_chunks(s)
                    last_before, last_between = quad_chunks(s, LAST_CHUNKS)
                    if not first:
                        if s == LAST_QUAD_STEP:
                            inverse_std(a, NQ - 1)
                        mix_chunks(a, last_before + last_between)
                        if s == TOTAL_STEP:
                            layer1_std(a)
                            if is_zero(a):
                                pool.wait_ge(s_w1, 4 * 4 * HO * 16)
                            layer1_mix(a)
                    if not last:
                        if s == QUAD_STEP[0] and not first:
                            pool.wait_ge(s_red1, 2 * U1 * b)
                        mix_chunks(b, before)
                        if s in QUAD_STEP:
                            inverse_std(b, QUAD_STEP.index(s))
                        mix_chunks(b, between)

            nc.gpsimd.memset(w1[:, :, :, :, :], 0.0).then_inc(s_zero, 1)
            nc.gpsimd.memset(prod_g[:, 0:P], 0.0).then_inc(s_zero, 1)
            nc.gpsimd.memset(expo[:, :], -0.5).then_inc(s_zero, 1)
            pool.wait_ge(s_zero, 3)
            for k in range(W0_STEPS):
                pool.wait_ge(s_wst, 8 * (k + 1))
                for dst, src in w0_scatter(k, (2, 3)):
                    nc.gpsimd.dma_start(dst, src).then_inc(s_w0p[k % 2], 16)
            for scattered in (*s_w0, *s_w0p):
                pool.wait_ge(scattered, W0_STEPS // 2 * 8 * 16)
            body(0, True, False)
            body(1, False, False)
            with pool.Fori(2, B) as b:
                body(b, False, False)
            body(B, False, True)


_INS = ["x", "L0_conv_coeff_real", "L0_conv_coeff_imag", "L0_conv_proj",
        "L1_conv_w1_real", "L1_conv_w1_imag", "L1_conv_w2_real", "L1_conv_w2_imag"]


def kernel(**inputs):
    import numpy as _np
    import concourse.bacc as _bacc
    from concourse import mybir as _mybir
    from concourse.bass_utils import run_bass_kernel_spmd as _run

    nc = _bacc.Bacc("TRN2", target_bir_lowering=False, num_devices=1, dynamic_dma_scratch_size=1024)
    arrays, args = {}, []
    for name, a in [(n, inputs[n]) for n in _INS] + [("table", constants())]:
        a = _np.ascontiguousarray(a)
        arrays[f"in_{name}_dram"] = a
        args.append(nc.dram_tensor(f"in_{name}_dram", a.shape, _mybir.dt.from_np(a.dtype), kind="ExternalInput").ap())
    args.append(nc.dram_tensor("out_0_dram", (B, C, H, W), _mybir.dt.float32, kind="ExternalOutput").ap())
    conv_preact_two_layers(nc, *args)
    r = _run(nc, [arrays], core_ids=[0])
    return r.results[0]["out_0_dram"]
```
